# Optimizing a Trainium2 kernel written in Bass

```python
import numpy as np
import jax
import jax.numpy as jnp

def _softmax(x, axis=-1):
    return jax.nn.softmax(x, axis=axis)

def _gelu(x):
    return jax.nn.gelu(x, approximate=True)

def _silu(x):
    return jax.nn.silu(x)

def _sigmoid(x):
    return jax.nn.sigmoid(x)

def _layernorm(x, axis=-1, eps=1e-05):
    m = jnp.mean(x, axis=axis, keepdims=True)
    v = jnp.var(x, axis=axis, keepdims=True)
    return (x - m) / jnp.sqrt(v + eps)

def _scatter_add(tgt, idx, src, axis=0):
    return tgt.at[idx].add(src)

def _segment_sum(src, seg, n):
    return jax.ops.segment_sum(src, seg, n)
kernel_name = 'mk_gnn_ffn_d2_gnn_r8_283bef'

def setup_inputs(seed: int=0):
    np.random.seed(seed)
    _w = jnp.asarray

    def _rec_inputs():
        import jax
        import jax.numpy as jnp
        _gk = jax.random.key(seed)
        x = 0.5 + 0.2886 * jax.random.normal(jax.random.fold_in(_gk, 1), (1250, 1024), jnp.float32)
        src = jax.random.randint(jax.random.fold_in(_gk, 2), (20000,), 0, 1250, jnp.int32)
        dst = jnp.minimum((1250 * jax.random.uniform(jax.random.fold_in(_gk, 3), (20000,)) ** 2.0).astype(jnp.int32), 9999)
        _o = jnp.argsort(dst, stable=True)
        src = src[_o]
        dst = dst[_o]
        edge_weight = jax.random.uniform(jax.random.fold_in(_gk, 13), (20000,), jnp.float32, 0.0, 0.999998)
        return (x, src, dst, edge_weight)
    x, src, dst, edge_weight = _rec_inputs()

    def _L0_gnn_setup():
        import jax, jax.numpy as jnp
        import numpy as np
        N_NODES = 6250
        N_EDGES = 100000
        IN_SIZE = 1024
        EMB = 500
        key = jax.random.key(seed)
        ks = jax.random.split(key, 9)
        x = jax.random.uniform(ks[0], (N_NODES, IN_SIZE), dtype=jnp.float32)
        edge_index = jax.random.randint(ks[1], (2, N_EDGES), 0, N_NODES, dtype=jnp.int32)
        edge_weight = jax.random.uniform(ks[2], (N_EDGES,), dtype=jnp.float32)
        s = 0.05
        wenc = jax.random.normal(ks[3], (EMB, IN_SIZE), dtype=jnp.float32) * s
        benc = jax.random.normal(ks[4], (EMB,), dtype=jnp.float32) * s
        wdec = jax.random.normal(ks[5], (IN_SIZE, EMB), dtype=jnp.float32) * s
        bdec = jax.random.normal(ks[6], (IN_SIZE,), dtype=jnp.float32) * s
        conv_weight = jax.random.normal(ks[7], (EMB, EMB), dtype=jnp.float32) * 0.1
        lin_weight = jax.random.normal(ks[8], (EMB, EMB), dtype=jnp.float32) * 0.1 + jnp.eye(EMB, dtype=jnp.float32)
        return {'x': x, 'edge_index': edge_index, 'edge_weight': edge_weight, 'wenc': wenc, 'benc': benc, 'wdec': wdec, 'bdec': bdec, 'conv_weight': conv_weight, 'lin_weight': lin_weight}
    _L0_gnn_all = _L0_gnn_setup()
    _L0_gnn_in = {k: v for k, v in _L0_gnn_all.items() if k in ('wenc', 'benc', 'wdec', 'bdec', 'conv_weight', 'lin_weight')}
    del _L0_gnn_all

    def _L0_ffn_setup():
        import jax, jax.numpy as jnp
        import numpy as np
        INT8_MAX = 127.0

        def _absmax_scale(x, axes):
            amax = jnp.max(jnp.abs(x), axis=axes, keepdims=True)
            return jnp.maximum(amax, 1e-12) / INT8_MAX
        key = jax.random.key(seed)
        k1, k2 = jax.random.split(key)
        lhs = jax.random.normal(k1, (4, 1024, 1024), dtype=jnp.float32)
        rhs = jax.random.normal(k2, (1024, 1024), dtype=jnp.float32)
        return {'lhs': lhs, 'rhs': rhs}
    _L0_ffn_all = _L0_ffn_setup()
    _L0_ffn_in = {k: v for k, v in _L0_ffn_all.items() if k in ('rhs',)}
    del _L0_ffn_all

    def _L1_gnn_setup():
        import jax, jax.numpy as jnp
        import numpy as np
        N_DIAS = 64
        L = 60
        N = N_DIAS * L
        E = N_DIAS * L * (L - 1)
        D = 1024
        H = 512
        K = 4

        def _build_edges():
            idx = np.arange(L)
            src = np.repeat(idx, L)
            dst = np.tile(idx, L)
            m = src != dst
            src, dst = (src[m], dst[m])
            offs = (np.arange(N_DIAS) * L)[:, None]
            row = (src[None, :] + offs).reshape(-1)
            col = (dst[None, :] + offs).reshape(-1)
            return (row.astype(np.int32), col.astype(np.int32))
        key = jax.random.key(seed)
        k0, k1, k2 = jax.random.split(key, 3)
        row, col = _build_edges()
        return {'emotions_feat': jax.random.normal(k0, (N, D), jnp.float32), 'W1': jax.random.normal(k1, (D, H), jnp.float32) * 0.02, 'b1': jnp.zeros((H,), jnp.float32), 'Wg': jax.random.normal(k2, (K, 2 * H, 1), jnp.float32) * 0.02, 'bg': jnp.zeros((K, 1), jnp.float32), 'row': jnp.asarray(row), 'col': jnp.asarray(col)}
    _L1_gnn_all = _L1_gnn_setup()
    _L1_gnn_in = {k: v for k, v in _L1_gnn_all.items() if k in ('W1', 'b1', 'Wg', 'bg')}
    del _L1_gnn_all

    def _L1_ffn_setup():
        import jax, jax.numpy as jnp
        import numpy as np
        DIM = 1024

        def _reference_tuple_inner(x, W_r, W_k, W_v, mu_r, mu_k):
            B, T, C = x.shape
            x_prev = jnp.concatenate([jnp.zeros((B, 1, C), x.dtype), x[:, :-1, :]], axis=1)
            xr = mu_r * x + (1.0 - mu_r) * x_prev
            xk = mu_k * x + (1.0 - mu_k) * x_prev
            r = jax.nn.sigmoid(jnp.einsum('btc,dc->btd', xr, W_r))
            k = jnp.einsum('btc,dc->btd', xk, W_k)
            k_act = jnp.square(jax.nn.relu(k))
            out = r * jnp.einsum('btc,dc->btd', k_act, W_v)
            new_state = x[:, -1, :]
            return (out, new_state)
        key = jax.random.key(seed)
        ks = jax.random.split(key, 6)
        B, T, C = (8, 256, DIM)
        x = jax.random.normal(ks[0], (B, T, C), dtype=jnp.float32)
        s = 1.0 / np.sqrt(C)
        W_r = jax.random.uniform(ks[1], (C, C), jnp.float32, -s, s)
        W_k = jax.random.uniform(ks[2], (C, C), jnp.float32, -s, s)
        W_v = jax.random.uniform(ks[3], (C, C), jnp.float32, -s, s)
        mu_r = jax.random.uniform(ks[4], (C,), jnp.float32)
        mu_k = jax.random.uniform(ks[5], (C,), jnp.float32)
        return {'x': x, 'W_r': W_r, 'W_k': W_k, 'W_v': W_v, 'mu_r': mu_r, 'mu_k': mu_k}
    _L1_ffn_all = _L1_ffn_setup()
    _L1_ffn_in = {k: v for k, v in _L1_ffn_all.items() if k in ('W_r', 'W_k', 'W_v', 'mu_r', 'mu_k')}
    del _L1_ffn_all
    return {'x': x, 'src': src, 'dst': dst, 'edge_weight': edge_weight, 'L0_gnn_wenc': _L0_gnn_in['wenc'], 'L0_gnn_benc': _L0_gnn_in['benc'], 'L0_gnn_wdec': _L0_gnn_in['wdec'], 'L0_gnn_bdec': _L0_gnn_in['bdec'], 'L0_gnn_conv_weight': _L0_gnn_in['conv_weight'], 'L0_gnn_lin_weight': _L0_gnn_in['lin_weight'], 'L0_ffn_rhs': _L0_ffn_in['rhs'], 'L1_gnn_W1': _L1_gnn_in['W1'], 'L1_gnn_b1': _L1_gnn_in['b1'], 'L1_gnn_Wg': _L1_gnn_in['Wg'], 'L1_gnn_bg': _L1_gnn_in['bg'], 'L1_ffn_W_r': _L1_ffn_in['W_r'], 'L1_ffn_W_k': _L1_ffn_in['W_k'], 'L1_ffn_W_v': _L1_ffn_in['W_v'], 'L1_ffn_mu_r': _L1_ffn_in['mu_r'], 'L1_ffn_mu_k': _L1_ffn_in['mu_k']}

def reference(x, src, dst, edge_weight, L0_gnn_wenc, L0_gnn_benc, L0_gnn_wdec, L0_gnn_bdec, L0_gnn_conv_weight, L0_gnn_lin_weight, L0_ffn_rhs, L1_gnn_W1, L1_gnn_b1, L1_gnn_Wg, L1_gnn_bg, L1_ffn_W_r, L1_ffn_W_k, L1_ffn_W_v, L1_ffn_mu_r, L1_ffn_mu_k):
    import jax
    import jax.numpy as jnp

    def _L0_gnn_ref(x, edge_index, edge_weight, wenc, benc, wdec, bdec, conv_weight, lin_weight):
        import jax, jax.numpy as jnp
        import numpy as np
        N_NODES = 6250
        N_EDGES = 100000
        IN_SIZE = 1024
        EMB = 500
        h = jax.nn.sigmoid(x @ wenc.T + benc)
        h2 = h @ conv_weight
        src, dst = (edge_index[0], edge_index[1])
        msgs = h2[src] * edge_weight[:, None]
        agg = jax.ops.segment_sum(msgs, dst, num_segments=x.shape[0])
        hout = agg + h @ lin_weight.T
        p = hout @ wdec.T + bdec
        return p

    def _L0_ffn_ref(lhs, rhs):
        import jax, jax.numpy as jnp
        import numpy as np
        INT8_MAX = 127.0

        def _absmax_scale(x, axes):
            amax = jnp.max(jnp.abs(x), axis=axes, keepdims=True)
            return jnp.maximum(amax, 1e-12) / INT8_MAX
        lhs_scale = _absmax_scale(lhs, (2,))
        rhs_scale = _absmax_scale(rhs, (0,))
        q_lhs = jnp.clip(jnp.round(lhs / lhs_scale), -INT8_MAX, INT8_MAX).astype(jnp.int8)
        q_rhs = jnp.clip(jnp.round(rhs / rhs_scale), -INT8_MAX, INT8_MAX).astype(jnp.int8)
        acc = jax.lax.dot_general(q_lhs, q_rhs, (((2,), (0,)), ((), ())), preferred_element_type=jnp.int32)
        return acc.astype(jnp.float32) * lhs_scale * rhs_scale

    def _L1_gnn_ref(emotions_feat, W1, b1, Wg, bg, row, col):
        import jax, jax.numpy as jnp
        import numpy as np
        N_DIAS = 64
        L = 60
        N = N_DIAS * L
        E = N_DIAS * L * (L - 1)
        D = 1024
        H = 512
        K = 4

        def _build_edges():
            idx = np.arange(L)
            src = np.repeat(idx, L)
            dst = np.tile(idx, L)
            m = src != dst
            src, dst = (src[m], dst[m])
            offs = (np.arange(N_DIAS) * L)[:, None]
            row = (src[None, :] + offs).reshape(-1)
            col = (dst[None, :] + offs).reshape(-1)
            return (row.astype(np.int32), col.astype(np.int32))
        n = emotions_feat.shape[0]
        x1 = emotions_feat @ W1 + b1
        h = x1.shape[1]
        deg = jax.ops.segment_sum(jnp.ones_like(col, x1.dtype), col, num_segments=n)
        dis = jnp.clip(deg, 1.0) ** (-0.5)
        norm = dis[row] * dis[col]
        gnn = x1
        for k in range(Wg.shape[0]):
            Wi, Wj = (Wg[k, :h], Wg[k, h:])
            x_i = gnn[col]
            x_j = gnn[row]
            alpha = jnp.tanh(x_i @ Wi + x_j @ Wj + bg[k])
            msg = norm[:, None] * alpha * x_j
            agg = jax.ops.segment_sum(msg, col, num_segments=n)
            gnn = gnn + agg
        return jnp.concatenate([x1, gnn], axis=1)

    def _L1_ffn_ref(x, W_r, W_k, W_v, mu_r, mu_k):
        import jax, jax.numpy as jnp
        import numpy as np
        DIM = 1024

        def _reference_tuple_inner(x, W_r, W_k, W_v, mu_r, mu_k):
            B, T, C = x.shape
            x_prev = jnp.concatenate([jnp.zeros((B, 1, C), x.dtype), x[:, :-1, :]], axis=1)
            xr = mu_r * x + (1.0 - mu_r) * x_prev
            xk = mu_k * x + (1.0 - mu_k) * x_prev
            r = jax.nn.sigmoid(jnp.einsum('btc,dc->btd', xr, W_r))
            k = jnp.einsum('btc,dc->btd', xk, W_k)
            k_act = jnp.square(jax.nn.relu(k))
            out = r * jnp.einsum('btc,dc->btd', k_act, W_v)
            new_state = x[:, -1, :]
            return (out, new_state)
        return _reference_tuple_inner(x, W_r, W_k, W_v, mu_r, mu_k)[0]
    edge_index = jnp.stack([src, dst])
    x = x + _L0_gnn_ref(_layernorm(x, axis=-1), edge_index, edge_weight, L0_gnn_wenc, L0_gnn_benc, L0_gnn_wdec, L0_gnn_bdec, L0_gnn_conv_weight, L0_gnn_lin_weight)
    x = x + _L0_ffn_ref(_layernorm(x, axis=-1)[None], L0_ffn_rhs)[0]
    x = x + _L1_gnn_ref(_layernorm(x, axis=-1), L1_gnn_W1, L1_gnn_b1, L1_gnn_Wg, L1_gnn_bg, src, dst)
    x = x + _L1_ffn_ref(_layernorm(x, axis=-1)[None], L1_ffn_W_r, L1_ffn_W_k, L1_ffn_W_v, L1_ffn_mu_r, L1_ffn_mu_k)[0]
    return x

_drawn_inputs = setup_inputs


def setup_inputs(seed=0):
    import zlib

    import numpy as np

    out = dict(_drawn_inputs(seed))
    spreads = {'L1_gnn_b1': (0.0, 2.0), 'L1_gnn_bg': (0.0, 2.0)}
    factors = {'L0_gnn_benc': 3.034,
     'L0_gnn_bdec': 5.691,
     'L1_gnn_Wg': 36.442,
     'L1_ffn_W_r': 8.0,
     'L1_ffn_W_k': 8.0,
     'L1_ffn_W_v': 8.0,
     'L1_ffn_mu_r': 8.0,
     'L1_ffn_mu_k': 8.0}
    for name, (base, spread) in spreads.items():
        noise = np.random.default_rng([zlib.crc32(name.encode()), seed]).standard_normal(out[name].shape)
        drawn = base * np.exp(spread * noise) if base else spread * noise
        out[name] = jnp.asarray(drawn.astype(out[name].dtype))
    for name, factor in factors.items():
        out[name] = (out[name] * factor).astype(out[name].dtype)
    return out
```

```python
from contextlib import ExitStack

import concourse.bass as bass
from concourse import mybir

F32 = mybir.dt.float32
BF16 = mybir.dt.bfloat16
I32 = mybir.dt.int32
ALU = mybir.AluOpType
ACT = mybir.ActivationFunctionType
AX = mybir.AxisListType

N, D, E = 1250, 1024, 20000
TN = 125
NT = N // TN
CH = E // TN
EMB = 500
MB = EMB // TN
KD = D // 128
H = 512
STEPS = 4
W = 25
NWIN = N // W
PADN = N + W
HALF = 512
MAGIC = float(3 << 22)
EPS = 1e-5
COLS = [(0, 418), (418, 416), (834, 416)]
GROUPS = [(0, 4), (4, 4), (8, 2)]
PAIRS = NT // 2
PN = 2 * TN
ARENA = 52124


def build(nc, x, src, dst, edge_w, wenc_t, benc, wdec_t, bdec, conv, lin_t, rhs, W1, b1, Wg, bg,
          Wr_t, Wk_t, Wv_t, mu_r, mu_k, out):
    with ExitStack() as ctx:
        def sem(name):
            return ctx.enter_context(nc.semaphore(name))

        def sb(name, shape, dt=F32):
            return ctx.enter_context(nc.sbuf_tensor(name, shape, dt))

        arena = sb("arena", [128, ARENA])

        def at(off, n, rows=TN):
            return arena[0:rows, off:off + n]

        def tiles(off, a, b, rows=TN):
            return at(off, a * b, rows).rearrange("p (a b) -> p a b", b=b)

        edges = tiles(0, 2 * NT, PADN)
        counts = edges[:, NT:2 * NT, :]
        X = tiles(0, NT, D)
        o_tail = NT * D
        raw2 = [at(o_tail + b * D, D, 128) for b in range(2)]
        xT = tiles(o_tail, KD, TN, 128)
        o_a = 2 * NT * PADN
        xlnT = tiles(o_a, KD, N, 128)
        h2 = tiles(o_a, NT, EMB)
        qT = at(o_a, NT * KD * TN // 2, 128).bitcast(BF16).rearrange("p (t k n) -> p t k n", t=NT, k=KD)
        gB = tiles(o_a, NT, H)
        o_b = o_a + NT * H
        houtT = tiles(o_b, MB, N)
        gA = tiles(o_b, NT, H)
        o_c = o_b + NT * H
        wenc = tiles(o_c, KD, EMB, 128)
        wdec = tiles(o_c, MB, D)
        w1 = tiles(o_c, KD, H, 128)
        mring = tiles(o_c, NT, 4 * TN)
        diag = tiles(o_c + NT * 4 * TN, NT, TN)
        o_d = o_c + KD * H
        hT = tiles(o_d, MB, N)
        qR = at(o_d, KD * D // 2, 128).bitcast(BF16).rearrange("p (k n) -> p k n", k=KD)
        o_e = o_d + NT * H
        xin = [at(o_e + b * D, D) for b in range(2)]
        y = [at(o_e + (2 + b) * D, D) for b in range(2)]
        convw = tiles(o_e, MB, EMB)
        linw = tiles(o_e + 2 * D, MB, EMB)
        raw1 = [at(o_e + b * D, D, 128) for b in range(2)]
        qtile = at(o_e, D // 2).bitcast(BF16)
        b1_row = at(o_e, H)
        tmp = [at(o_e + D + b * H, H) for b in range(2)]
        o_f = o_e + 4 * D
        bdec_row = at(o_f, D)
        rs_row = at(o_f + D, D, 128)
        inv_row = at(o_f + 2 * D, D, 128)
        wg_row = [at(o_f + b * D, D) for b in range(2)]
        deg_pick = tiles(o_f + D, NT, TN)

        def columns(i, k=1):
            return at(o_f + i * CH, k * CH)

        e_int = columns(0, 2).bitcast(I32).rearrange("p (a c) -> p a c", a=2)
        e_f = columns(2, 2).rearrange("p (a c) -> p a c", a=2)
        e_w = columns(4)
        w_part = columns(5, 3).rearrange("p (a c) -> p a c", a=3)
        src_lo, s0, s1, s2, key0, key = (columns(8 + i) for i in range(6))
        base_i = columns(14).bitcast(I32)
        extremes = at(o_d, 2 * CH).rearrange("p (a c) -> p a c", a=2)
        reduced = at(o_d + 2 * CH, 2 * CH).rearrange("p (a c) -> p a c", a=2)
        lo_hot = [at(o_d + 1000 + b * 252, 252).bitcast(BF16).rearrange("p (a s) -> p a s", a=4) for b in range(2)]
        win_hot = [at(o_d + 1600 + b * NT * W // 2, NT * W // 2).bitcast(BF16) for b in range(2)]

        wk_off = [o_tail, o_tail + D] + [o_d + 2154 + i * D for i in range(3)] + \
                 [o_e + 2 * D, o_e + 3 * D, o_f + 2 * D]
        wk = [at(o, D, 128) for o in wk_off]
        o_l = o_tail + 2 * D
        wr = tiles(o_l, KD, D, 128)
        wv = tiles(o_l + KD * D, KD, D, 128)
        o_m = o_l + 2 * KD * D
        xl = tiles(o_m, KD, PN + 1, 128)
        xkT = tiles(o_m + 2008, KD, PN, 128)
        xrT = tiles(o_m + 4008, KD, PN, 128)
        kact = tiles(o_m + 6008, KD, PN, 128)
        gate = [at(o_m + 8008 + b * D, D) for b in range(2)]
        yl = [at(o_m + 10056 + b * D, D) for b in range(2)]
        mixt = [at(o_m + 12104 + b * PN, PN, 128) for b in range(2)]
        last_col = at(o_m + 12604, KD, 128)
        prod = tmp
        assert o_m + 12612 <= wk_off[2] and wk_off[4] + D <= o_e + D and o_f + 3 * D <= ARENA

        ident = sb("ident", [128, 128])
        identb = sb("identb", [128, 128], BF16)
        ones = sb("ones", [128, 128])
        iota = sb("iota", [128, NT * W], BF16)
        win_start = sb("win_start", [128, NWIN])
        st = sb("st", [128, 12])
        mv = sb("mv", [128, 2])
        std = sb("std", [128, 1])
        rstd = sb("rstd", [128, 1])
        eps = sb("eps", [128, 1])
        flag = sb("flag", [128, 4])
        npass_i = sb("npass_i", [128, 1], I32)
        benc_c = sb("benc_c", [128, MB])
        deg_c = sb("deg_c", [128, NT])
        dis_c = sb("dis_c", [128, NT])
        amax = sb("amax", [128, 1])
        lscale = sb("lscale", [128, NT])
        linv = sb("linv", [128, 1])
        qscale = sb("qscale", [128, 1])
        dot_a = sb("dot_a", [128, NT])
        dot_b = sb("dot_b", [128, NT])
        bias_b = sb("bias_b", [128, NT])
        bg_row = sb("bg_row", [128, STEPS])
        mu = sb("mu", [128, 4, KD])

        ps = ctx.enter_context(nc.psum_tensor("ps", [128, 8, HALF], F32))

        def bank(i, n=HALF, rows=TN, o=0):
            return ps[0:rows, i, o:o + n]

        def tile_of(a, t):
            return a[:, bass.ds(t, 1), :].rearrange("p a d -> p (a d)")

        ld_edges, ld_enc, ld_convlin, ld_dec = sem("ld_edges"), sem("ld_enc"), sem("ld_convlin"), sem("ld_dec")
        ld_x = [sem("ld_x0"), sem("ld_x1")]
        ld_X = [sem("ld_Xa"), sem("ld_Xb")]
        ld_raw1 = [sem("ld_raw1_0"), sem("ld_raw1_1")]
        ld_raw2 = [sem("ld_raw2_0"), sem("ld_raw2_1")]
        ld_w1, ld_b1, ld_small, ld_bdec = sem("ld_w1"), sem("ld_b1"), sem("ld_small"), sem("ld_bdec")
        ld_wg = [sem("ld_wg0"), sem("ld_wg1")]
        ld_wk, ld_wr, ld_wv = sem("ld_wk"), sem("ld_wr"), sem("ld_wv")
        consts = sem("consts")
        ln_var, ln_std, ln_step, ln_out = sem("ln_var"), sem("ln_std"), sem("ln_step"), sem("ln_out")
        turned, turned_out = sem("turned"), sem("turned_out")
        prep, prep_max, npass_set, window_set = sem("prep"), sem("prep_max"), sem("npass_set"), sem("window_set")
        hot_ready, chunk_sum, chunk_added, edges_done = (sem("hot_ready"), sem("chunk_sum"), sem("chunk_added"),
                                                         sem("edges_done"))
        deg_sum, deg_col, deg_root, dis_set = sem("deg_sum"), sem("deg_col"), sem("deg_root"), sem("dis_set")
        dis_diag, dis_row, norm_set = sem("dis_diag"), sem("dis_row"), sem("norm_set")
        mm, mm_out = sem("mm"), sem("mm_out")
        dec_mm, dec_out, xb_ready = sem("dec_mm"), sem("dec_out"), sem("xb_ready")
        rabs, rmax, rmax_all, rscale, rmul, rround, rq = (sem("rabs"), sem("rmax"), sem("rmax_all"), sem("rscale"), sem("rmul"),
                                                    sem("rround"), sem("rq"))
        q_step, q_turned, q_copied = sem("q_step"), sem("q_turned"), sem("q_copied")
        int_mm, int_scaled, x2_ready = sem("int_mm"), sem("int_scaled"), sem("x2_ready")
        g0_mm, g0_out, g0_added, dots = sem("g0_mm"), sem("g0_out"), sem("g0_added"), sem("dots")
        bias_set, diag_set, a_row, tanh_out = sem("bias_set"), sem("diag_set"), sem("a_row"), sem("tanh_out")
        m_set, slot_free, g_mm, g_out, x3_ready = (sem("m_set"), sem("slot_free"), sem("g_mm"), sem("g_out"),
                                                   sem("x3_ready"))
        mu_set, part_mix, mix_k, mix_r = sem("mu_set"), sem("part_mix"), sem("mix_k"), sem("mix_r")
        last_kept, pair_turned, pair_copied, col_set = (sem("last_kept"), sem("pair_turned"), sem("pair_copied"),
                                                        sem("col_set"))
        k_mm, k_relu, k_sq = sem("k_mm"), sem("k_relu"), sem("k_sq")
        r_mm, r_out, v_mm, v_prod, y_out = sem("r_mm"), sem("r_out"), sem("v_mm"), sem("v_prod"), sem("y_out")
        stored = sem("stored")

        x_t = x.rearrange("(t p) d -> p t d", p=TN)
        out_t = out.rearrange("(t p) d -> p t d", p=TN)
        rhs_t = rhs.rearrange("(k p) n -> p k n", p=128)

        NG = 12 + NT + 12
        NM = STEPS * len(GROUPS) * NT

        block = ctx.enter_context(nc.Block())

        @block.sync
        def _(sp):
            sp.dma_start(e_int[:, 0, :], src).then_inc(ld_edges, 16)
            sp.dma_start(e_int[:, 1, :], dst).then_inc(ld_edges, 16)
            sp.dma_start(e_w, edge_w).then_inc(ld_edges, 16)
            with sp.Fori(0, NT - 1, 2) as t:
                for b in range(2):
                    sp.wait_ge(ln_out, t)
                    sp.dma_start(xin[b], tile_of(x_t, t + b)).then_inc(ld_x[b], 16)
            sp.dma_start(wenc, wenc_t.rearrange("(k p) m -> p k m", p=128)).then_inc(ld_enc, 16)
            sp.dma_start(benc_c[0:TN, :], benc).then_inc(ld_enc, 16)
            sp.dma_start(bg_row[0:TN, :], bg.partition_broadcast(TN)).then_inc(ld_small, 16)
            sp.dma_start(mu[:, 0, :], mu_k).then_inc(ld_small, 16)
            sp.dma_start(mu[:, 1, :], mu_r).then_inc(ld_small, 16)
            sp.wait_ge(turned, 2 * NT)
            sp.dma_start(convw, conv.rearrange("(k p) m -> p k m", p=TN)).then_inc(ld_convlin, 16)
            sp.dma_start(linw, lin_t.rearrange("(k p) m -> p k m", p=TN)).then_inc(ld_convlin, 16)
            sp.wait_ge(edges_done, 1)
            sp.dma_start(bdec_row, bdec.partition_broadcast(TN)).then_inc(ld_bdec, 16)
            sp.wait_ge(mm, 12)
            sp.dma_start(wdec, wdec_t.rearrange("(k p) m -> p k m", p=TN)).then_inc(ld_dec, 16)
            sp.wait_ge(mm, 12 + NT)
            with sp.Fori(0, KD - 1, 2) as k:
                for b in range(2):
                    sp.wait_ge(rmax, k)
                    sp.dma_start(raw1[b], tile_of(rhs_t, k + b)).then_inc(ld_raw1[b], 16)
            sp.wait_ge(mm, NG)
            for half in range(2):
                part = slice(half * NT // 2, (half + 1) * NT // 2)
                sp.dma_start(X[:, part, :], x_t[:, part, :]).then_inc(ld_X[half], 16)
            with sp.Fori(0, KD - 1, 2) as k:
                for b in range(2):
                    sp.wait_ge(rq, k)
                    sp.dma_start(raw2[b], tile_of(rhs_t, k + b)).then_inc(ld_raw2[b], 16)
            sp.wait_ge(dec_mm, 2 * NT)
            sp.dma_start(w1, W1.rearrange("(k p) m -> p k m", p=128)).then_inc(ld_w1, 16)
            sp.wait_ge(q_turned, NT)
            sp.dma_start(b1_row, b1.partition_broadcast(TN)).then_inc(ld_b1, 16)
            sp.wait_ge(xb_ready, NT)
            sp.dma_start(wg_row[0], Wg[0].partition_broadcast(TN)).then_inc(ld_wg[0], 16)
            sp.wait_ge(int_scaled, 2 * NT)
            sp.dma_start(wg_row[1], Wg[1].partition_broadcast(TN)).then_inc(ld_wg[1], 16)
            sp.wait_ge(g0_out, NT)
            for k in range(KD):
                sp.dma_start(wk[k], Wk_t[k * 128:(k + 1) * 128, :]).then_inc(ld_wk, 16)
            for k in range(2, STEPS):
                sp.wait_ge(dots, 2 * NT * (k - 1))
                sp.dma_start(wg_row[k % 2], Wg[k].partition_broadcast(TN)).then_inc(ld_wg[k % 2], 16)
            sp.wait_ge(slot_free, NM)
            sp.wait_ge(g_out, STEPS * NT)
            sp.dma_start(wr, Wr_t.rearrange("(k p) m -> p k m", p=128)).then_inc(ld_wr, 16)
            sp.dma_start(wv, Wv_t.rearrange("(k p) m -> p k m", p=128)).then_inc(ld_wv, 16)
            with sp.Fori(0, NT) as t:
                sp.wait_ge(y_out, 2 * t + 2)
                sp.dma_start(tile_of(out_t, t), tile_of(X, t)).then_inc(stored, 16)
            sp.wait_ge(stored, 16 * NT)

        @block.gpsimd
        def _(pool):
            pool.memset(eps[:], EPS).then_inc(consts, 1)
            pool.memset(ones[:], 1.0).then_inc(consts, 1)
            pool.memset(ident[:], 0.0).then_inc(consts, 1)
            pool.memset(identb[:], 0.0).then_inc(consts, 1)
            pool.wait_ge(consts, 4)
            for m in (ident, identb):
                pool.affine_select(out=m[:], in_=m[:], compare_op=ALU.not_equal, fill=1.0, base=0,
                                   pattern=[[-1, 128]], channel_multiplier=1).then_inc(consts, 1)
            pool.iota(iota[:], [[1, NT * W]], base=0, channel_multiplier=0,
                      allow_small_or_imprecise_dtypes=True).then_inc(consts, 1)
            pool.iota(win_start[:], [[W, NWIN]], base=0, channel_multiplier=0,
                      allow_small_or_imprecise_dtypes=True).then_inc(consts, 1)
            pool.memset(edges[:, 0:NT, :], 0.0).then_inc(chunk_added, 1)
            pool.memset(edges[:, NT:, :], 0.0).then_inc(chunk_added, 1)
            pool.wait_ge(prep, 3)
            pool.partition_all_reduce(reduced, extremes, TN, bass.bass_isa.ReduceOp.max).then_inc(prep_max, 1)
            pool.wait_ge(rmax, KD)
            pool.partition_all_reduce(inv_row, rs_row, 128, bass.bass_isa.ReduceOp.absmax).then_inc(rmax_all, 1)

            def add_bdec(half):
                pool.wait_ge(ld_bdec, 16)
                pool.wait_ge(ld_X[half], 16)
                with pool.Fori(0, NT // 2) as t:
                    xt = tile_of(X, t + half * (NT // 2))
                    pool.tensor_tensor(xt, xt, bdec_row, ALU.add).then_inc(xb_ready, 1)

            add_bdec(0)
            pool.wait_ge(rscale, 2)
            for k in range(KD):
                pool.wait_ge(ld_raw2[k % 2], 16 * (k // 2 + 1))
                pool.tensor_tensor(raw2[k % 2], raw2[k % 2], inv_row, ALU.mult).then_inc(rmul, 1)
            add_bdec(1)
            with pool.Fori(0, NT) as t:
                pool.wait_ge(g0_out, t + 1)
                xt = X[:, bass.ds(t, 1), 0:H].rearrange("p a d -> p (a d)")
                pool.tensor_tensor(xt, xt, tile_of(gA, t), ALU.add).then_inc(g0_added, 1)
            with pool.Fori(0, NT) as t:
                pool.wait_ge(g_out, (STEPS - 1) * NT + t + 1)
                xt = X[:, bass.ds(t, 1), H:D].rearrange("p a d -> p (a d)")
                pool.tensor_tensor(xt, xt, tile_of(gA, t), ALU.add).then_inc(x3_ready, 1)
            with pool.Fori(0, PAIRS) as c:
                for d in range(KD):
                    pool.wait_ge(k_relu, c * KD + d + 1)
                    pool.tensor_tensor(kact[:, d, :], kact[:, d, :], kact[:, d, :], ALU.mult).then_inc(k_sq, 1)

        @block.vector
        def _(dve):
            def stats(xt, n):
                dve.bn_stats(st[0:TN, 0:6], xt[:, 0:HALF]).then_inc(ln_step, 1)
                dve.bn_stats(st[0:TN, 6:12], xt[:, HALF:D]).then_inc(ln_step, 1)
                dve.wait_ge(ln_step, n * 3 + 2)
                dve.bn_aggr(mv[0:TN, :], st[0:TN, :]).then_inc(ln_var, 1)
                dve.wait_ge(ln_std, n + 1)
                dve.reciprocal(rstd[0:TN, :], std[0:TN, :]).then_inc(ln_step, 1)
                dve.wait_ge(ln_step, n * 3 + 3)

            def normalise(dst_ap, xt):
                dve.tensor_scalar(dst_ap, xt, mv[0:TN, 0:1], rstd[0:TN, :],
                                  ALU.subtract, ALU.mult).then_inc(ln_out, 1)

            dve.wait_ge(consts, 8)
            for t in range(NT):
                b = t % 2
                dve.wait_ge(ld_x[b], 16 * (t // 2 + 1))
                stats(xin[b], t)
                if t >= 2:
                    dve.wait_ge(turned, 2 * t - 2)
                normalise(y[b], xin[b])

            count = [0]

            def then(ins):
                count[0] += 1
                ins.then_inc(prep, 1)
                dve.wait_ge(prep, count[0])

            dve.wait_ge(ld_edges, 48)
            then(dve.tensor_copy(e_f, e_int))
            then(dve.tensor_copy(extremes[:, 0, :], e_f[:, 1, :]))
            then(dve.tensor_scalar(extremes[:, 1, :], e_f[:, 1, :], -1.0, None, ALU.mult))
            then(dve.tensor_scalar(s0, e_f[:, 0, :], 1.0 / TN, 0.5 / TN - 0.5, ALU.mult, ALU.add))
            then(dve.tensor_scalar(s1, s0, MAGIC, None, ALU.add))
            then(dve.tensor_scalar(s2, s1, -MAGIC, None, ALU.add))
            then(dve.scalar_tensor_tensor(src_lo, s2, -float(TN), e_f[:, 0, :], ALU.mult, ALU.add))
            then(dve.tensor_scalar(key0, s2, float(W), 1.0, ALU.mult, ALU.add))
            rest = e_w
            for p in range(3):
                as_bf16 = win_hot[0][:, 0:CH]
                then(dve.tensor_copy(as_bf16, rest))
                then(dve.tensor_copy(w_part[:, p, :], as_bf16))
                if p < 2:
                    left = [s0, s1][p]
                    then(dve.tensor_tensor(left, rest, w_part[:, p, :], ALU.subtract))
                    rest = left
            dve.wait_ge(prep_max, 1)
            then(dve.tensor_tensor(s0, reduced[:, 0, :], reduced[:, 1, :], ALU.add))
            then(dve.tensor_reduce(flag[0:TN, 0:1], s0, AX.X, ALU.max))
            then(dve.tensor_scalar(flag[0:TN, 1:2], flag[0:TN, 0:1], W - 0.5, None, ALU.is_lt))
            then(dve.tensor_scalar(flag[0:TN, 2:3], flag[0:TN, 1:2], -float(NWIN - 1), float(NWIN),
                                   ALU.mult, ALU.add))
            dve.tensor_copy(npass_i[0:TN, :], flag[0:TN, 2:3]).then_inc(npass_set, 1)
            then(dve.tensor_scalar(s1, reduced[:, 1, :], -1.0, flag[0:TN, 1:2], ALU.mult, ALU.mult))
            then(dve.tensor_scalar(flag[0:TN, 3:4], flag[0:TN, 1:2], -1.0, 1.0, ALU.mult, ALU.add))
            dve.wait_ge(npass_set, 1)
            npass = dve.value_load(npass_i[0:1, 0:1], min_val=1, max_val=NWIN)

            def hots(c, b):
                for p in range(3):
                    dve.tensor_scalar(lo_hot[b][:, p, 0:TN], iota[0:TN, 0:TN], src_lo[:, bass.ds(c, 1)],
                                      w_part[:, p, bass.ds(c, 1)], ALU.is_equal, ALU.mult)
                dve.tensor_scalar(lo_hot[b][:, 3, 0:TN], iota[0:TN, 0:TN], src_lo[:, bass.ds(c, 1)], None,
                                  ALU.is_equal)
                dve.tensor_scalar(win_hot[b], iota[0:TN, :], key[:, bass.ds(c, 1)], None,
                                  ALU.is_equal).then_inc(hot_ready, 1)

            def add_chunk(c, b, i):
                start = dve.value_load(base_i[0:1, bass.ds(c, 1)], min_val=0, max_val=N - 1)
                dve.wait_ge(chunk_sum, i + 1)
                dve.wait_ge(chunk_added, i + 2)
                window = edges[:, :, bass.ds(start, W)]
                dve.tensor_tensor(window, bank(4 + b, 2 * NT * W).rearrange("p (a w) -> p a w", w=W),
                                  window, ALU.add).then_inc(chunk_added, 1)

            with dve.Fori(0, npass) as j:
                in_pass = [0]

                def step(ins):
                    in_pass[0] += 1
                    ins.then_inc(window_set, 1)
                    dve.wait_ge(window_set, j * 9 + in_pass[0])

                step(dve.tensor_scalar(flag[0:TN, 0:1], win_start[0:TN, bass.ds(j, 1)], flag[0:TN, 3:4], None,
                                       ALU.mult))
                step(dve.tensor_scalar(s2, s1, flag[0:TN, 0:1], None, ALU.add))
                step(dve.tensor_copy(base_i, s2))
                step(dve.tensor_tensor(s0, e_f[:, 1, :], s2, ALU.subtract))
                step(dve.tensor_scalar(s2, s0, -0.5, None, ALU.is_gt))
                step(dve.scalar_tensor_tensor(s2, s0, W - 0.5, s2, ALU.is_lt, ALU.mult))
                step(dve.tensor_tensor(s0, s0, key0, ALU.add))
                step(dve.tensor_tensor(s0, s0, s2, ALU.mult))
                step(dve.tensor_scalar(key, s0, -1.0, None, ALU.add))
                hots(0, 0)
                with dve.Fori(0, CH - 2, 2) as c:
                    for b in range(2):
                        hots(c + b + 1, 1 - b)
                        add_chunk(c + b, b, j * CH + c + b)
                hots(CH - 1, 1)
                for b in range(2):
                    add_chunk(CH - 2 + b, b, j * CH + CH - 2 + b)
            dve.wait_ge(chunk_added, npass * CH + 2)
            dve.memset(flag[0:TN, 0:1], 0.0).then_inc(edges_done, 1)

            dve.wait_ge(deg_sum, 1)
            for t in range(NT):
                dve.tensor_tensor_reduce(deg_pick[:, t, :], bank(5 + t // 4, TN, TN, (t % 4) * TN),
                                         ident[0:TN, 0:TN], 1.0, 0.0, ALU.mult, ALU.add,
                                         deg_c[0:TN, t:t + 1]).then_inc(deg_col, 1)
            dve.wait_ge(deg_col, NT)
            dve.tensor_scalar(deg_c[0:TN, :], deg_c[0:TN, :], 1.0, None, ALU.max).then_inc(deg_col, 1)
            dve.wait_ge(deg_root, 1)
            dve.reciprocal(dis_c[0:TN, :], deg_c[0:TN, :]).then_inc(dis_set, 1)
            dve.wait_ge(dis_set, 1)
            for t in range(NT):
                dve.tensor_scalar(deg_pick[:, t, :], ident[0:TN, 0:TN], dis_c[0:TN, t:t + 1], None,
                                  ALU.mult).then_inc(dis_diag, 1)
            dve.wait_ge(dis_row, 1)
            for g, (t0, k) in enumerate(GROUPS):
                with dve.Fori(0, NT) as s:
                    part = counts[:, bass.ds(s, 1), t0 * TN:(t0 + k) * TN].rearrange("p a n -> p (a n)")
                    dve.scalar_tensor_tensor(part, part, dis_c[0:TN, bass.ds(s, 1)], bank(5 + g, k * TN),
                                             ALU.mult, ALU.mult).then_inc(norm_set, 1)

            for k in range(KD):
                dve.wait_ge(rabs, k + 1)
                if k == 0:
                    dve.tensor_copy(rs_row, raw1[0]).then_inc(rmax, 1)
                else:
                    dve.wait_ge(rmax, k)
                    dve.tensor_tensor(rs_row, raw1[k % 2], rs_row, ALU.max).then_inc(rmax, 1)
            dve.wait_ge(rmax_all, 1)
            dve.tensor_scalar(rs_row, inv_row, 1e-12, 1.0 / 127.0, ALU.max, ALU.mult).then_inc(rscale, 1)
            dve.wait_ge(rscale, 1)
            dve.reciprocal(inv_row, rs_row).then_inc(rscale, 1)

            def round_rhs(k):
                dve.wait_ge(rmul, k + 1)
                dve.tensor_scalar(raw2[k % 2], raw2[k % 2], MAGIC, None, ALU.add).then_inc(rround, 1)
                dve.wait_ge(rround, k + 1)
                dve.tensor_scalar(qR[:, k, :], raw2[k % 2], -MAGIC, None, ALU.add).then_inc(rq, 1)

            for k in range(KD):
                round_rhs(k)

            for t in range(NT):
                xt = X[:, t, :]
                dve.wait_ge(xb_ready, t + 1)
                for h in range(2):
                    dve.wait_ge(dec_mm, 2 * t + h + 1)
                    xh = xt[:, h * HALF:(h + 1) * HALF]
                    dve.tensor_tensor(xh, bank(2 * (t % 2) + h), xh, ALU.add).then_inc(dec_out, 1)
                dve.wait_ge(dec_out, 2 * t + 2)
                stats(xt, t + NT)
                dve.wait_ge(q_step, 6 * t)
                normalise(y[0], xt)
                dve.wait_ge(ln_out, t + NT + 1)
                dve.tensor_reduce(amax[0:TN, :], y[0], AX.X, ALU.max,
                                  apply_absolute_value=True).then_inc(q_step, 1)
                dve.wait_ge(q_step, 6 * t + 1)
                dve.tensor_scalar(qscale[0:TN, :], amax[0:TN, :], 1e-12, 1.0 / 127.0, ALU.max, ALU.mult).then_inc(q_step, 1)
                dve.wait_ge(q_step, 6 * t + 2)
                dve.reciprocal(linv[0:TN, :], qscale[0:TN, :]).then_inc(q_step, 1)
                dve.tensor_copy(lscale[0:TN, t:t + 1], qscale[0:TN, :]).then_inc(q_step, 1)
                dve.wait_ge(q_step, 6 * t + 4)
                dve.tensor_scalar(y[0], y[0], linv[0:TN, :], MAGIC, ALU.mult, ALU.add).then_inc(q_step, 1)
                dve.wait_ge(q_step, 6 * t + 5)
                dve.wait_ge(q_turned, t)
                dve.tensor_scalar(qtile, y[0], -MAGIC, None, ALU.add).then_inc(q_step, 1)

            def dot_products(gt, k, t):
                for i, (dot, junk) in enumerate(((dot_a, tmp[0]), (dot_b, tmp[1]))):
                    dve.tensor_tensor_reduce(junk, gt, wg_row[k % 2][:, i * H:(i + 1) * H], 1.0, 0.0,
                                             ALU.mult, ALU.add, dot[0:TN, t:t + 1]).then_inc(dots, 1)

            def integer_tile(t):
                if t > 2:
                    dve.wait_ge(dots, 2 * t - 4)
                for h in range(2):
                    dve.wait_ge(int_mm, 2 * t + h + 1)
                    if t:
                        dve.wait_ge(x2_ready, 2 * t + h - 1)
                    dve.scalar_tensor_tensor(tmp[h], bank(h), lscale[0:TN, t:t + 1],
                                             rs_row[0:TN, h * HALF:(h + 1) * HALF], ALU.mult,
                                             ALU.mult).then_inc(int_scaled, 1)
                    dve.wait_ge(int_scaled, 2 * t + h + 1)
                    xh = X[:, t, h * HALF:(h + 1) * HALF]
                    dve.tensor_tensor(xh, xh, tmp[h], ALU.add).then_inc(x2_ready, 1)
                dve.wait_ge(x2_ready, 2 * t + 2)
                stats(X[:, t, :], t + 2 * NT)
                dve.wait_ge(turned, 2 * NT + 2 * t)
                normalise(y[1], X[:, t, :])

            def graph_input(t):
                dve.wait_ge(g0_mm, t + 1)
                dve.tensor_tensor(gA[:, t, :], bank(4), b1_row, ALU.add).then_inc(g0_out, 1)
                dve.wait_ge(g0_out, t + 1)
                dve.wait_ge(x2_ready, 2 * min(t + 3, NT))
                dve.wait_ge(dots, 2 * t)
                dot_products(gA[:, t, :], 0, t)

            dve.wait_ge(ld_wg[0], 16)
            dve.wait_ge(ld_b1, 16)
            dve.wait_ge(q_step, 6 * NT)
            integer_tile(0)
            integer_tile(1)
            for t in range(2, NT):
                integer_tile(t)
                graph_input(t - 2)
            graph_input(NT - 2)
            graph_input(NT - 1)

            dve.wait_ge(ld_small, 48)
            for k in range(STEPS):
                g_in, g_next = (gA, gB) if k % 2 == 0 else (gB, gA)

                def matrix_parts(g):
                    t0, cnt = GROUPS[g]
                    with dve.Fori(0, NT) as s:
                        dve.wait_ge(tanh_out, s + (k * len(GROUPS) + g) * NT + 1)
                        m = mring[:, bass.ds(s, 1), 0:cnt * TN].rearrange("p a n -> p (a n)")
                        c = counts[:, bass.ds(s, 1), t0 * TN:(t0 + cnt) * TN].rearrange("p a n -> p (a n)")
                        dve.tensor_tensor(m, m, c, ALU.mult).then_inc(m_set, 1)

                def new_state(g):
                    t0, cnt = GROUPS[g]
                    for t in range(t0, t0 + cnt):
                        if t < t0 + cnt - 1:
                            dve.wait_ge(g_mm, k * (NT - len(GROUPS)) + t - g + 1)
                        else:
                            dve.wait_ge(slot_free, (k * len(GROUPS) + g + 1) * NT)
                        dve.tensor_tensor(g_next[:, t, :], bank(t % 5), g_in[:, t, :], ALU.add).then_inc(g_out, 1)
                    if k + 1 < STEPS:
                        for t in range(t0, t0 + cnt):
                            dve.wait_ge(g_out, k * NT + t + 1)
                            dve.wait_ge(dots, 2 * ((k + 1) * NT + t))
                            dot_products(g_next[:, t, :], k + 1, t)

                dve.wait_ge(dots, 2 * NT * (k + 1))
                dve.tensor_scalar(bias_b[0:TN, :], dot_b[0:TN, :], bg_row[0:TN, k:k + 1], None,
                                  ALU.add).then_inc(bias_set, 1)
                with dve.Fori(0, NT) as t:
                    dve.tensor_scalar(tile_of(diag, t), ident[0:TN, 0:TN], dot_a[0:TN, bass.ds(t, 1)], None,
                                      ALU.mult).then_inc(diag_set, 1)
                matrix_parts(0)
                matrix_parts(1)
                if k + 1 < STEPS:
                    dve.wait_ge(ld_wg[(k + 1) % 2], 16 * ((k + 1) // 2 + 1))
                if k == 1:
                    dve.wait_ge(g0_added, NT)
                new_state(0)
                matrix_parts(2)
                new_state(1)
                new_state(2)

            dve.wait_ge(x3_ready, NT)
            dve.tensor_scalar(mu[:, 2:4, :], mu[:, 0:2, :], -1.0, 1.0, ALU.mult, ALU.add).then_inc(mu_set, 1)
            dve.memset(last_col, 0.0).then_inc(last_kept, 1)

            def pair_norm(c):
                for b in range(2):
                    xt = X[:, 2 * c + b, :]
                    stats(xt, 2 * c + b + 3 * NT)
                    dve.wait_ge(pair_turned, 4 * c)
                    normalise(yl[b], xt)

            def pair_mix(c):
                for i, (mixed, ready) in enumerate(((xkT, mix_k), (xrT, mix_r))):
                    if i == 0:
                        dve.wait_ge(k_mm, KD * c)
                    else:
                        dve.wait_ge(r_mm, 4 * c)
                    for k in range(KD):
                        dve.wait_ge(part_mix, 2 * KD * c + i * KD + k + 1)
                        dve.scalar_tensor_tensor(mixed[:, k, :], xl[:, k, 1:PN + 1], mu[:, i, k:k + 1],
                                                 mixt[k % 2], ALU.mult, ALU.add).then_inc(ready, 1)

            def pair_out(c):
                for b in range(2):
                    for h in range(2):
                        n = 4 * c + 2 * b + h
                        dve.wait_ge(v_mm, n + 1)
                        dve.wait_ge(r_out, n + 1)
                        dve.wait_ge(y_out, 4 * c + max(2 * b + h - 1, 0))
                        dve.tensor_tensor(prod[h], bank(6 + h), gate[b][:, h * HALF:(h + 1) * HALF],
                                          ALU.mult).then_inc(v_prod, 1)
                        dve.wait_ge(v_prod, n + 1)
                        xh = X[:, 2 * c + b, h * HALF:(h + 1) * HALF]
                        dve.tensor_tensor(xh, xh, prod[h], ALU.add).then_inc(y_out, 1)

            pair_norm(0)
            pair_mix(0)
            for c in range(PAIRS - 1):
                pair_norm(c + 1)
                pair_mix(c + 1)
                pair_out(c)
            pair_out(PAIRS - 1)

        @block.scalar
        def _(act):
            def root(n):
                act.wait_ge(ln_var, n + 1)
                act.activation(std[0:TN, :], mv[0:TN, 1:2], ACT.Sqrt, bias=eps[0:TN, :]).then_inc(ln_std, 1)

            act.wait_ge(consts, 8)
            with act.Fori(0, NT - 1, 2) as t:
                for b in range(2):
                    root(t + b)
                    for half in range(2):
                        act.wait_ge(turned, 2 * t + 2 * b + half + 1)
                        act.activation(
                            xlnT[:, 4 * half:4 * half + 4, bass.ds((t + b) * TN, TN)],
                            bank(2 * b + half, 4 * TN, 128).rearrange("p (k n) -> p k n", k=4),
                            ACT.Copy).then_inc(turned_out, 1)
            act.wait_ge(deg_col, NT + 1)
            act.activation(deg_c[0:TN, :], deg_c[0:TN, :], ACT.Sqrt).then_inc(deg_root, 1)
            act.wait_ge(ld_enc, 32)
            n = 0
            for c0, cn in COLS:
                for m in range(MB):
                    act.wait_ge(mm, n + 1)
                    act.activation(hT[:, m, c0:c0 + cn], bank(n % 4, cn), ACT.Sigmoid,
                                   bias=benc_c[0:TN, m:m + 1]).then_inc(mm_out, 1)
                    n += 1
            for t in range(NT):
                act.wait_ge(mm, n + 1)
                act.activation(h2[:, t, :], bank(n % 4, EMB), ACT.Copy).then_inc(mm_out, 1)
                n += 1
            for m in range(MB):
                if m < KD // 4:
                    for k in range(4 * m, 4 * m + 4):
                        act.wait_ge(ld_raw1[k % 2], 16 * (k // 2 + 1))
                        act.activation(raw1[k % 2], raw1[k % 2], ACT.Abs).then_inc(rabs, 1)
                for c0, cn in COLS:
                    act.wait_ge(mm, n + 1)
                    act.activation(houtT[:, m, c0:c0 + cn], bank(n % 4, cn), ACT.Copy).then_inc(mm_out, 1)
                    n += 1

            def q_copy(t):
                act.wait_ge(q_turned, t + 1)
                turned_q = ps[:, 4, :].bitcast(BF16)[:, 0:KD * 126].rearrange("p (k n) -> p k n", k=KD)
                act.activation(qT[:, bass.ds(t, 1), :, :].rearrange("p t k n -> p (t k) n"),
                               turned_q[:, :, 0:TN], ACT.Copy).then_inc(q_copied, 1)

            root(NT)
            with act.Fori(0, NT - 1) as t:
                root(t + NT + 1)
                q_copy(t)
            q_copy(NT - 1)

            def x_copy(t):
                for half in range(2):
                    act.wait_ge(g0_mm, t)
                    act.wait_ge(turned, 2 * NT + 2 * t + half + 1)
                    act.activation(xT[:, 4 * half:4 * half + 4, :],
                                   bank(2 + half, 4 * TN, 128).rearrange("p (k n) -> p k n", k=4),
                                   ACT.Copy).then_inc(turned_out, 1)

            act.wait_ge(rq, KD)
            root(2 * NT)
            with act.Fori(0, NT - 1) as t:
                root(t + 2 * NT + 1)
                x_copy(t)
            x_copy(NT - 1)

            with act.Fori(0, STEPS) as k:
                act.wait_ge(bias_set, k + 1)
                act.wait_ge(a_row, k + 1)
                for g, (t0, cnt) in enumerate(GROUPS):
                    with act.Fori(0, NT) as s:
                        if g == 0:
                            act.wait_ge(slot_free, k * (len(GROUPS) * NT))
                        else:
                            act.wait_ge(slot_free, k * (len(GROUPS) * NT) + (g - 1) * NT + s + 1)
                        m = mring[:, bass.ds(s, 1), 0:cnt * TN].rearrange("p a n -> p (a n)")
                        act.activation(m, bank(5 + g, cnt * TN), ACT.Tanh,
                                       bias=bias_b[0:TN, bass.ds(s, 1)]).then_inc(tanh_out, 1)

            def pair_copy(c):
                for b in range(2):
                    for half in range(2):
                        act.wait_ge(pair_turned, 4 * c + 2 * b + half + 1)
                        act.activation(xl[:, 4 * half:4 * half + 4, 1 + b * TN:1 + (b + 1) * TN],
                                       bank(2 * b + half, 4 * TN, 128).rearrange("p (k n) -> p k n", k=4),
                                       ACT.Copy).then_inc(pair_copied, 1)
                act.wait_ge(last_kept, c + 1)
                act.activation(xl[:, :, 0], last_col, ACT.Copy).then_inc(col_set, 1)

            def mix_terms(c):
                act.wait_ge(pair_copied, 4 * c + 4)
                act.wait_ge(col_set, c + 1)
                for i, ready in enumerate((mix_k, mix_r)):
                    for k in range(KD):
                        if k >= 2:
                            act.wait_ge(ready, KD * c + k - 1)
                        elif i == 1:
                            act.wait_ge(mix_k, KD * c + KD)
                        else:
                            act.wait_ge(mix_r, KD * c)
                        act.activation(mixt[k % 2], xl[:, k, 0:PN], ACT.Copy,
                                       scale=mu[:, 2 + i, k:k + 1]).then_inc(part_mix, 1)
                act.wait_ge(mix_r, KD * c + KD)
                act.activation(last_col, xl[:, :, PN], ACT.Copy).then_inc(last_kept, 1)

            def pair_out(c):
                act.wait_ge(v_mm, 4 * c)
                for d in range(KD):
                    act.wait_ge(k_mm, KD * c + d + 1)
                    act.activation(kact[:, d, :], bank(d % 4, PN, 128), ACT.Relu).then_inc(k_relu, 1)
                act.wait_ge(v_prod, 4 * c)
                for b in range(2):
                    for h in range(2):
                        act.wait_ge(r_mm, 4 * c + 2 * b + h + 1)
                        act.activation(gate[b][:, h * HALF:(h + 1) * HALF], bank(4 + h),
                                       ACT.Sigmoid).then_inc(r_out, 1)

            for b in range(2):
                root(3 * NT + b)
            act.wait_ge(mu_set, 1)
            pair_copy(0)
            mix_terms(0)
            with act.Fori(0, PAIRS - 1) as c:
                for b in range(2):
                    root(3 * NT + 2 * c + 2 + b)
                pair_out(c)
                pair_copy(c + 1)
                mix_terms(c + 1)
            pair_out(PAIRS - 1)

        @block.tensor
        def _(pe):
            def turn(tile, banks, done):
                for half in range(2):
                    for k in range(4):
                        f = 4 * half + k
                        t = pe.transpose(bank(banks[half], TN, 128, k * TN), tile[:, f * 128:(f + 1) * 128],
                                         ident[0:TN, 0:TN])
                    t.then_inc(done, 1)

            pe.wait_ge(consts, 8)
            with pe.Fori(0, NT - 1, 2) as t:
                for b in range(2):
                    pe.wait_ge(ln_out, t + b + 1)
                    pe.wait_ge(turned_out, 2 * t)
                    turn(y[b], (2 * b, 2 * b + 1), turned)

            pe.wait_ge(npass_set, 1)
            npass = pe.value_load(npass_i[0:1, 0:1], min_val=1, max_val=NWIN)
            with pe.Fori(0, npass) as j:
                with pe.Fori(0, CH, 2) as c:
                    for b in range(2):
                        pe.wait_ge(hot_ready, j * CH + c + b + 1)
                        pe.wait_ge(chunk_added, j * CH + c + b + 1)
                        for p in range(3):
                            pe.matmul(bank(4 + b, NT * W), lo_hot[b][:, p, 0:TN], win_hot[b],
                                      start=(p == 0), stop=(p == 2), skip_group_check=True)
                        pe.matmul(bank(4 + b, NT * W, TN, NT * W), lo_hot[b][:, 3, 0:TN], win_hot[b],
                                  start=False, stop=True, skip_group_check=True).then_inc(chunk_sum, 1)

            pe.wait_ge(chunk_added, npass * CH + 2)
            for g, (t0, k) in enumerate(GROUPS):
                for s in range(NT):
                    last = pe.matmul(bank(5 + g, k * TN), ones[0:TN, 0:TN],
                                     counts[:, s, t0 * TN:(t0 + k) * TN], start=(s == 0), stop=(s == NT - 1))
            last.then_inc(deg_sum, 1)

            pe.wait_ge(ld_enc, 32)
            pe.wait_ge(turned_out, 2 * NT)
            n = 0
            for c0, cn in COLS:
                for m in range(MB):
                    if n >= 4:
                        pe.wait_ge(mm_out, n - 3)
                    for k in range(KD):
                        last = pe.matmul(bank(n % 4, cn), wenc[:, k, m * TN:(m + 1) * TN],
                                         xlnT[:, k, c0:c0 + cn], start=(k == 0), stop=(k == KD - 1))
                    last.then_inc(mm, 1)
                    n += 1
                    if n == 2:
                        pe.wait_ge(dis_diag, NT)
                        for t in range(NT):
                            last = pe.matmul(bank(5 + t // 4, TN, TN, (t % 4) * TN), ones[0:TN, 0:TN],
                                             deg_pick[:, t, :], start=True, stop=True, skip_group_check=True)
                        last.then_inc(dis_row, 1)
            pe.wait_ge(ld_convlin, 32)
            pe.wait_ge(mm_out, 12)
            for t in range(NT):
                pe.wait_ge(mm_out, n - 3)
                for k in range(MB):
                    last = pe.matmul(bank(n % 4, EMB), hT[:, k, t * TN:(t + 1) * TN], convw[:, k, :],
                                     start=(k == 0), stop=(k == MB - 1))
                last.then_inc(mm, 1)
                n += 1
            pe.wait_ge(mm_out, n)
            for m in range(MB):
                for c0, cn in COLS:
                    pe.wait_ge(mm_out, n - 3)
                    for k in range(MB):
                        pe.matmul(bank(n % 4, cn), linw[:, k, m * TN:(m + 1) * TN], hT[:, k, c0:c0 + cn],
                                  start=(k == 0), stop=False)
                    for s in range(NT):
                        last = pe.matmul(bank(n % 4, cn), h2[:, s, m * TN:(m + 1) * TN],
                                         edges[:, s, c0:c0 + cn], start=False, stop=(s == NT - 1))
                    last.then_inc(mm, 1)
                    n += 1

            def turn_q(t):
                pe.wait_ge(q_step, 6 * t + 6)
                if t:
                    pe.wait_ge(q_copied, t)
                for f in range(KD):
                    last = pe.transpose(ps[:, 4, :].bitcast(BF16)[:, f * 126:f * 126 + TN],
                                        qtile[:, f * 128:(f + 1) * 128], identb[0:TN, 0:TN])
                last.then_inc(q_turned, 1)

            pe.wait_ge(ld_dec, 16)
            pe.wait_ge(mm_out, NG)
            for t in range(NT):
                for h in range(2):
                    if t >= 2:
                        pe.wait_ge(dec_out, 2 * (t - 2) + h + 1)
                    for k in range(MB):
                        last = pe.matmul(bank(2 * (t % 2) + h), houtT[:, k, t * TN:(t + 1) * TN],
                                         wdec[:, k, h * HALF:(h + 1) * HALF], start=(k == 0), stop=(k == MB - 1))
                    last.then_inc(dec_mm, 1)
                if t:
                    turn_q(t - 1)
            turn_q(NT - 1)

            def integer_product(t):
                pe.wait_ge(q_copied, t + 1)
                pe.wait_ge(int_scaled, 2 * t)
                for h in range(2):
                    for k in range(KD):
                        lhs = qT[:, bass.ds(t, 1), k, :].rearrange("p t n -> p (t n)")
                        last = pe.matmul(bank(h), lhs, qR[:, k, h * HALF:(h + 1) * HALF],
                                         start=(k == 0), stop=(k == KD - 1))
                    last.then_inc(int_mm, 1)

            def graph_input(t):
                pe.wait_ge(turned_out, 2 * NT + 2 * t + 2)
                pe.wait_ge(g0_out, t)
                for k in range(KD):
                    last = pe.matmul(bank(4), xT[:, k, :], w1[:, k, :], start=(k == 0), stop=(k == KD - 1))
                last.then_inc(g0_mm, 1)

            def turn_x(t):
                pe.wait_ge(ln_out, 2 * NT + t + 1)
                pe.wait_ge(turned_out, 2 * NT + 2 * t)
                turn(y[1], (2, 3), turned)

            pe.wait_ge(rq, KD)
            pe.wait_ge(dec_out, 2 * NT)
            integer_product(0)
            integer_product(1)
            turn_x(0)
            pe.wait_ge(ld_w1, 16)
            with pe.Fori(2, NT) as t:
                integer_product(t)
                graph_input(t - 2)
                turn_x(t - 1)
            graph_input(NT - 2)
            turn_x(NT - 1)
            graph_input(NT - 1)

            pe.wait_ge(g0_out, NT)
            with pe.Fori(0, STEPS, 2) as k2:
                for i in range(2):
                    k = k2 + i
                    g_in = (gA, gB)[i]
                    pe.wait_ge(diag_set, k * NT + NT)
                    pe.wait_ge(tanh_out, k * (len(GROUPS) * NT))
                    for t in range(NT):
                        last = pe.matmul(bank(5 + t // 4, TN, TN, (t % 4) * TN), ones[0:TN, 0:TN], diag[:, t, :],
                                         start=True, stop=True, skip_group_check=True)
                    last.then_inc(a_row, 1)
                    for g, (t0, cnt) in enumerate(GROUPS):
                        for s in range(NT):
                            pe.wait_ge(m_set, k * (len(GROUPS) * NT) + g * NT + s + 1)
                            for d in range(cnt):
                                t = t0 + d
                                if s == 0 and t >= 5:
                                    pe.wait_ge(g_out, k * NT + t - 4)
                                last = pe.matmul(bank(t % 5), mring[:, s, d * TN:(d + 1) * TN], g_in[:, s, :],
                                                 start=(s == 0), stop=(s == NT - 1))
                                if s == NT - 1 and d < cnt - 1:
                                    last.then_inc(g_mm, 1)
                            last.then_inc(slot_free, 1)

            def turn_pair(c):
                for b in range(2):
                    pe.wait_ge(ln_out, 2 * c + 3 * NT + b + 1)
                    turn(yl[b], (2 * b, 2 * b + 1), pair_turned)

            def pair_products(c, more):
                pe.wait_ge(pair_copied, 4 * c + 4)
                for d in range(KD):
                    if d >= 4:
                        pe.wait_ge(k_relu, KD * c + d - 3)
                    for k in range(KD):
                        if d == 0:
                            pe.wait_ge(mix_k, KD * c + k + 1)
                        last = pe.matmul(bank(d % 4, PN, 128), wk[k][:, d * 128:(d + 1) * 128], xkT[:, k, :],
                                         start=(k == 0), stop=(k == KD - 1))
                    last.then_inc(k_mm, 1)
                for b in range(2):
                    for h in range(2):
                        pe.wait_ge(r_out, 4 * c + max(2 * b + h - 1, 0))
                        for k in range(KD):
                            if b == 0 and h == 0:
                                pe.wait_ge(mix_r, KD * c + k + 1)
                            last = pe.matmul(bank(4 + h), xrT[:, k, b * TN:(b + 1) * TN],
                                             wr[:, k, h * HALF:(h + 1) * HALF], start=(k == 0), stop=(k == KD - 1))
                        last.then_inc(r_mm, 1)
                if more:
                    pe.wait_ge(k_relu, KD * c + KD)
                    turn_pair(c + 1)
                for b in range(2):
                    for h in range(2):
                        pe.wait_ge(v_prod, 4 * c + max(2 * b + h - 1, 0))
                        for d in range(KD):
                            if b == 0 and h == 0:
                                pe.wait_ge(k_sq, KD * c + d + 1)
                            last = pe.matmul(bank(6 + h), kact[:, d, b * TN:(b + 1) * TN],
                                             wv[:, d, h * HALF:(h + 1) * HALF], start=(d == 0), stop=(d == KD - 1))
                        last.then_inc(v_mm, 1)

            pe.wait_ge(g_out, STEPS * NT)
            turn_pair(0)
            pe.wait_ge(ld_wk, 16 * KD)
            pe.wait_ge(ld_wr, 16)
            pe.wait_ge(ld_wv, 16)
            with pe.Fori(0, PAIRS - 1) as c:
                pair_products(c, True)
            pair_products(PAIRS - 1, False)


def kernel(x, src, dst, edge_weight, L0_gnn_wenc, L0_gnn_benc, L0_gnn_wdec, L0_gnn_bdec, L0_gnn_conv_weight,
           L0_gnn_lin_weight, L0_ffn_rhs, L1_gnn_W1, L1_gnn_b1, L1_gnn_Wg, L1_gnn_bg, L1_ffn_W_r, L1_ffn_W_k,
           L1_ffn_W_v, L1_ffn_mu_r, L1_ffn_mu_k):
    import numpy as np
    import concourse.bacc as bacc
    from concourse.bass_utils import run_bass_kernel_spmd

    def chunks(a):
        return np.asarray(a).reshape(CH, TN).T

    def blocks(a, p):
        return np.asarray(a).reshape(-1, p).T

    arrays = {
        "x": x, "src": chunks(src), "dst": chunks(dst), "edge_w": chunks(edge_weight),
        "wenc_t": np.asarray(L0_gnn_wenc).T, "benc": blocks(L0_gnn_benc, TN),
        "wdec_t": np.asarray(L0_gnn_wdec).T, "bdec": L0_gnn_bdec,
        "conv": L0_gnn_conv_weight, "lin_t": np.asarray(L0_gnn_lin_weight).T, "rhs": L0_ffn_rhs,
        "W1": L1_gnn_W1, "b1": L1_gnn_b1, "Wg": np.asarray(L1_gnn_Wg).reshape(STEPS, 2 * H),
        "bg": np.asarray(L1_gnn_bg).reshape(STEPS),
        "Wr_t": np.asarray(L1_ffn_W_r).T, "Wk_t": np.asarray(L1_ffn_W_k).T, "Wv_t": np.asarray(L1_ffn_W_v).T,
        "mu_r": blocks(L1_ffn_mu_r, 128), "mu_k": blocks(L1_ffn_mu_k, 128),
    }
    arrays = {k: np.ascontiguousarray(v) for k, v in arrays.items()}
    nc = bacc.Bacc("TRN2", target_bir_lowering=False, num_devices=1)
    args = {k: nc.dram_tensor(f"in_{k}", v.shape, mybir.dt.from_np(v.dtype), kind="ExternalInput").ap()
            for k, v in arrays.items()}
    args["out"] = nc.dram_tensor("out_x", (N, D), F32, kind="ExternalOutput").ap()
    build(nc, **args)
    got = run_bass_kernel_spmd(nc, [{f"in_{k}": v for k, v in arrays.items()}], core_ids=[0])
    return got.results[0]["out_x"]
```

```python
from contextlib import ExitStack

import concourse.bass as bass
from concourse import mybir

F32 = mybir.dt.float32
BF16 = mybir.dt.bfloat16
I32 = mybir.dt.int32
ALU = mybir.AluOpType
ACT = mybir.ActivationFunctionType
AX = mybir.AxisListType

N, D, E = 1250, 1024, 20000
TN = 125
NT = N // TN
CH = E // TN
EMB = 500
MB = EMB // TN
KD = D // 128
H = 512
STEPS = 4
W = 25
NWIN = N // W
PADN = N + W
HALF = 512
MAGIC = float(3 << 22)
EPS = 1e-5
COLS = [(0, 418), (418, 416), (834, 416)]
SLOTS = 4
DENSE = 3 * MB * KD + NT * MB
X_PARTS = [(0, 1), (1, 2), (3, 7)]
GROUPS = [(0, 4), (4, 4), (8, 2)]
PAIRS = NT // 2
PN = 2 * TN
ARENA = 52350


def group_end(n):
    return KD * min(n + 1, 12) + MB * max(n + 1 - 12, 0)


def build(nc, x, src, dst, edge_w, wenc_t, benc, wdec_t, bdec, conv, lin_t, rhs, W1, b1, Wg, bg,
          Wr_t, Wk_t, Wv_t, mu_r, mu_k, out):
    with ExitStack() as ctx:
        def sem(name):
            return ctx.enter_context(nc.semaphore(name))

        def sb(name, shape, dt=F32):
            return ctx.enter_context(nc.sbuf_tensor(name, shape, dt))

        arena = sb("arena", [128, ARENA])

        def at(off, n, rows=TN):
            return arena[0:rows, off:off + n]

        def tiles(off, a, b, rows=TN):
            return at(off, a * b, rows).rearrange("p (a b) -> p a b", b=b)

        edges = tiles(0, 2 * NT, PADN)
        counts = edges[:, NT:2 * NT, :]
        X = tiles(0, NT, D)
        o_tail = NT * D
        raw2 = [at(o_tail + b * D, D, 128) for b in range(2)]
        xT = tiles(o_tail, KD, TN, 128)
        o_a = 2 * NT * PADN
        xlnT = tiles(o_a, KD, N, 128)
        h2 = tiles(o_a, NT, EMB)
        qT = at(o_a, NT * KD * TN // 2, 128).bitcast(BF16).rearrange("p (t k n) -> p t k n", t=NT, k=KD)
        gB = tiles(o_a, NT, H)
        o_b = o_a + NT * H
        houtT = tiles(o_b, MB, N)
        gA = tiles(o_b, NT, H)
        o_c = o_b + NT * H
        wenc = tiles(o_c, KD, EMB, 128)
        wdec = tiles(o_c, MB, D)
        w1 = tiles(o_c, KD, H, 128)
        mring = tiles(o_c, NT, 4 * TN)
        diag = tiles(o_c + NT * 4 * TN, NT, TN)
        o_d = o_c + KD * H
        hT = tiles(o_d, MB, N)
        qR = at(o_d, KD * D // 2, 128).bitcast(BF16).rearrange("p (k n) -> p k n", k=KD)
        o_e = o_d + NT * H
        xin = [at(o_e + b * D, D) for b in range(2)]
        y = [at(o_e + (2 + b) * D, D) for b in range(2)]
        convw = tiles(o_e, MB, EMB)
        linw = tiles(o_e + 2 * D, MB, EMB)
        raw1 = [at(o_e + b * D, D, 128) for b in range(2)]
        qtile = at(o_e, D // 2).bitcast(BF16)
        b1_row = at(o_e, H)
        tmp = [at(o_e + D + b * H, H) for b in range(2)]
        o_f = o_e + 4 * D
        bdec_row = at(o_f, D)
        rs_row = at(o_f + D, D, 128)
        inv_row = at(o_f + 2 * D, D, 128)
        wg_row = [at(o_f + b * D, D) for b in range(2)]
        deg_sum_rows = at(o_f + 2 * D, N)
        dis_diags = tiles(o_f + 2 * D, NT, TN)

        def columns(i, k=1):
            return at(o_f + i * CH, k * CH)

        e_int = columns(0, 2).bitcast(I32).rearrange("p (a c) -> p a c", a=2)
        e_f = columns(2, 2).rearrange("p (a c) -> p a c", a=2)
        e_w = columns(4)
        w_part = columns(5, 3).rearrange("p (a c) -> p a c", a=3)
        src_lo, s0, s1, s2, key0, key = (columns(8 + i) for i in range(6))
        base_i = columns(14).bitcast(I32)
        extremes = at(o_d, 2 * CH).rearrange("p (a c) -> p a c", a=2)
        reduced = at(o_d + 2 * CH, 2 * CH).rearrange("p (a c) -> p a c", a=2)
        as_bf16 = at(o_d + 4 * CH, CH // 2).bitcast(BF16)
        lo_hot = at(o_e + 2 * D, SLOTS * 252).bitcast(BF16).rearrange("p (b a s) -> p b a s", b=SLOTS, a=4)
        win_hot = at(o_e + 2 * D + SLOTS * 252, SLOTS * 125).bitcast(BF16).rearrange("p (b w) -> p b w", b=SLOTS)

        wk_off = [o_tail, o_tail + D] + [o_d + 2154 + i * D for i in range(3)] + \
                 [o_e + 2 * D, o_e + 3 * D, o_f + 2 * D]
        wk = [at(o, D, 128) for o in wk_off]
        o_l = o_tail + 2 * D
        wr = tiles(o_l, KD, D, 128)
        wv = tiles(o_l + KD * D, KD, D, 128)
        o_m = o_l + 2 * KD * D
        xl = tiles(o_m, KD, PN + 1, 128)
        xkT = tiles(o_m + 2008, KD, PN, 128)
        xrT = tiles(o_m + 4008, KD, PN, 128)
        kact = tiles(o_m + 6008, KD, PN, 128)
        gate = [at(o_m + 8008 + b * D, D) for b in range(2)]
        yl = [at(o_m + 10056 + b * D, D) for b in range(2)]
        mixt = [at(o_m + 12104 + b * PN, PN, 128) for b in range(2)]
        last_col = at(o_m + 12604, KD, 128)
        prod = tmp
        assert o_m + 12612 <= wk_off[2] and wk_off[4] + D <= o_e + D and o_f + 3 * D <= ARENA

        ident = sb("ident", [128, 128])
        identb = sb("identb", [128, 128], BF16)
        ones = sb("ones", [128, 128])
        iota = sb("iota", [128, NT * W], BF16)
        win_start = sb("win_start", [128, NWIN])
        st = sb("st", [128, 12])
        mv = sb("mv", [128, 2])
        std = sb("std", [128, 1])
        rstd = sb("rstd", [128, 1])
        eps = sb("eps", [128, 1])
        flag = sb("flag", [128, 4])
        npass_i = sb("npass_i", [128, 1], I32)
        benc_c = sb("benc_c", [128, MB])
        deg_c = sb("deg_c", [128, NT])
        dis_c = sb("dis_c", [128, NT])
        amax = sb("amax", [128, 1])
        lscale = sb("lscale", [128, NT])
        linv = sb("linv", [128, 1])
        qscale = sb("qscale", [128, 1])
        dot_a = sb("dot_a", [128, NT])
        dot_b = sb("dot_b", [128, NT])
        bias_b = sb("bias_b", [128, NT])
        bg_row = sb("bg_row", [128, STEPS])
        mu = sb("mu", [128, 4, KD])

        ps = ctx.enter_context(nc.psum_tensor("ps", [128, 8, HALF], F32))

        def bank(i, n=HALF, rows=TN, o=0):
            return ps[0:rows, i, o:o + n]

        def tile_of(a, t):
            return a[:, bass.ds(t, 1), :].rearrange("p a d -> p (a d)")

        ld_edges, ld_enc, ld_conv, ld_lin, ld_dec = (sem("ld_edges"), sem("ld_enc"), sem("ld_conv"),
                                                       sem("ld_lin"), sem("ld_dec"))
        ld_x = [sem("ld_x0"), sem("ld_x1")]
        ld_X = [sem(f"ld_X{i}") for i in range(len(X_PARTS))]
        ld_raw1 = [sem("ld_raw1_0"), sem("ld_raw1_1")]
        ld_raw2 = [sem("ld_raw2_0"), sem("ld_raw2_1")]
        ld_w1, ld_b1, ld_small, ld_bdec = sem("ld_w1"), sem("ld_b1"), sem("ld_small"), sem("ld_bdec")
        ld_wg = [sem("ld_wg0"), sem("ld_wg1")]
        ld_wk, ld_wr, ld_wv = sem("ld_wk"), sem("ld_wr"), sem("ld_wv")
        consts = sem("consts")
        matrices_zero, plain_ready, part01_ready, part2_ready, deg_rows = (
            sem("matrices_zero"), sem("plain_ready"), sem("part01_ready"), sem("part2_ready"), sem("deg_rows"))
        ln_var, ln_std, ln_step, ln_out = sem("ln_var"), sem("ln_std"), sem("ln_step"), sem("ln_out")
        turned, turned_out = sem("turned"), sem("turned_out")
        prep, prep_max, npass_set, window_set = sem("prep"), sem("prep_max"), sem("npass_set"), sem("window_set")
        hot_ready, chunk_sum, chunk_added, edges_done = (sem("hot_ready"), sem("chunk_sum"), sem("chunk_added"),
                                                         sem("edges_done"))
        deg_sum, deg_col, deg_root, dis_set = sem("deg_sum"), sem("deg_col"), sem("deg_root"), sem("dis_set")
        dis_diag, dis_row, norm_set = sem("dis_diag"), sem("dis_row"), sem("norm_set")
        mm, mm_out = sem("mm"), sem("mm_out")
        dec_mm, dec_out, xb_ready = sem("dec_mm"), sem("dec_out"), sem("xb_ready")
        rabs, rmax, rmax_all, rscale, rmul, rround, rq = (sem("rabs"), sem("rmax"), sem("rmax_all"), sem("rscale"), sem("rmul"),
                                                    sem("rround"), sem("rq"))
        q_step, q_turned, q_copied = sem("q_step"), sem("q_turned"), sem("q_copied")
        int_mm, int_scaled, x2_ready = sem("int_mm"), sem("int_scaled"), sem("x2_ready")
        g0_mm, g0_out, g0_added, dots = sem("g0_mm"), sem("g0_out"), sem("g0_added"), sem("dots")
        bias_set, diag_set, a_row, tanh_out = sem("bias_set"), sem("diag_set"), sem("a_row"), sem("tanh_out")
        m_set, slot_free, g_mm, g_out, x3_ready = (sem("m_set"), sem("slot_free"), sem("g_mm"), sem("g_out"),
                                                   sem("x3_ready"))
        mu_set, part_mix, mix_k, mix_r = sem("mu_set"), sem("part_mix"), sem("mix_k"), sem("mix_r")
        last_kept, pair_turned, pair_copied, col_set = (sem("last_kept"), sem("pair_turned"), sem("pair_copied"),
                                                        sem("col_set"))
        k_mm, k_relu, k_sq = sem("k_mm"), sem("k_relu"), sem("k_sq")
        r_mm, r_out, v_mm, v_prod, y_out = sem("r_mm"), sem("r_out"), sem("v_mm"), sem("v_prod"), sem("y_out")
        stored = sem("stored")

        x_t = x.rearrange("(t p) d -> p t d", p=TN)
        out_t = out.rearrange("(t p) d -> p t d", p=TN)
        rhs_t = rhs.rearrange("(k p) n -> p k n", p=128)

        NG = 12 + NT + 12
        NM = STEPS * len(GROUPS) * NT

        block = ctx.enter_context(nc.Block())

        @block.sync
        def _(sp):
            sp.dma_start(e_int[:, 0, :], src).then_inc(ld_edges, 16)
            sp.dma_start(e_int[:, 1, :], dst).then_inc(ld_edges, 16)
            sp.dma_start(e_w, edge_w).then_inc(ld_edges, 16)
            for t in range(NT):
                if t >= 2:
                    sp.wait_ge(ln_out, t - 1)
                sp.dma_start(xin[t % 2], x_t[:, t, :]).then_inc(ld_x[t % 2], 16)
            sp.dma_start(wenc, wenc_t.rearrange("(k p) m -> p k m", p=128)).then_inc(ld_enc, 16)
            sp.dma_start(benc_c[0:TN, :], benc).then_inc(ld_enc, 16)
            sp.dma_start(bg_row[0:TN, :], bg.partition_broadcast(TN)).then_inc(ld_small, 16)
            sp.dma_start(mu[:, 0, :], mu_k).then_inc(ld_small, 16)
            sp.dma_start(mu[:, 1, :], mu_r).then_inc(ld_small, 16)
            sp.wait_ge(ln_out, NT)
            sp.dma_start(convw, conv.rearrange("(k p) m -> p k m", p=TN)).then_inc(ld_conv, 16)
            sp.wait_ge(edges_done, 1)
            sp.dma_start(linw, lin_t.rearrange("(k p) m -> p k m", p=TN)).then_inc(ld_lin, 16)
            sp.dma_start(bdec_row, bdec.partition_broadcast(TN)).then_inc(ld_bdec, 16)
            sp.wait_ge(mm, 12)
            sp.dma_start(wdec, wdec_t.rearrange("(k p) m -> p k m", p=TN)).then_inc(ld_dec, 16)
            sp.wait_ge(mm, 12 + NT)
            with sp.Fori(0, KD - 1, 2) as k:
                for b in range(2):
                    sp.wait_ge(rmax, k)
                    sp.dma_start(raw1[b], tile_of(rhs_t, k + b)).then_inc(ld_raw1[b], 16)
            sp.wait_ge(mm, NG)
            for i, (t0, k) in enumerate(X_PARTS):
                sp.dma_start(X[:, t0:t0 + k, :], x_t[:, t0:t0 + k, :]).then_inc(ld_X[i], 16)
            with sp.Fori(0, KD - 1, 2) as k:
                for b in range(2):
                    sp.wait_ge(rq, k)
                    sp.dma_start(raw2[b], tile_of(rhs_t, k + b)).then_inc(ld_raw2[b], 16)
            sp.wait_ge(dec_mm, 2 * NT)
            sp.dma_start(w1, W1.rearrange("(k p) m -> p k m", p=128)).then_inc(ld_w1, 16)
            sp.wait_ge(q_turned, NT)
            sp.dma_start(b1_row, b1.partition_broadcast(TN)).then_inc(ld_b1, 16)
            sp.wait_ge(xb_ready, NT)
            sp.dma_start(wg_row[0], Wg[0].partition_broadcast(TN)).then_inc(ld_wg[0], 16)
            sp.wait_ge(int_scaled, 2 * NT)
            sp.dma_start(wg_row[1], Wg[1].partition_broadcast(TN)).then_inc(ld_wg[1], 16)
            sp.wait_ge(g0_out, NT)
            for k in range(KD):
                sp.dma_start(wk[k], Wk_t[k * 128:(k + 1) * 128, :]).then_inc(ld_wk, 16)
            for k in range(2, STEPS):
                sp.wait_ge(dots, 2 * NT * (k - 1))
                sp.dma_start(wg_row[k % 2], Wg[k].partition_broadcast(TN)).then_inc(ld_wg[k % 2], 16)
            sp.wait_ge(slot_free, NM)
            sp.wait_ge(g_out, STEPS * NT)
            sp.dma_start(wr, Wr_t.rearrange("(k p) m -> p k m", p=128)).then_inc(ld_wr, 16)
            sp.dma_start(wv, Wv_t.rearrange("(k p) m -> p k m", p=128)).then_inc(ld_wv, 16)
            with sp.Fori(0, NT) as t:
                sp.wait_ge(y_out, 2 * t + 2)
                sp.dma_start(tile_of(out_t, t), tile_of(X, t)).then_inc(stored, 16)
            sp.wait_ge(stored, 16 * NT)

        @block.gpsimd
        def _(pool):
            pool.memset(eps[:], EPS).then_inc(consts, 1)
            pool.memset(ones[:], 1.0).then_inc(consts, 1)
            pool.memset(ident[:], 0.0).then_inc(consts, 1)
            pool.memset(identb[:], 0.0).then_inc(consts, 1)
            pool.wait_ge(consts, 4)
            for m in (ident, identb):
                pool.affine_select(out=m[:], in_=m[:], compare_op=ALU.not_equal, fill=1.0, base=0,
                                   pattern=[[-1, 128]], channel_multiplier=1).then_inc(consts, 1)
            pool.iota(iota[:], [[1, NT * W]], base=0, channel_multiplier=0,
                      allow_small_or_imprecise_dtypes=True).then_inc(consts, 1)
            pool.iota(win_start[:], [[W, NWIN]], base=0, channel_multiplier=0,
                      allow_small_or_imprecise_dtypes=True).then_inc(consts, 1)
            pool.wait_ge(prep, 3)
            pool.partition_all_reduce(reduced, extremes, TN, bass.bass_isa.ReduceOp.max).then_inc(prep_max, 1)
            pool.memset(edges[:, 0:NT, :], 0.0).then_inc(matrices_zero, 1)
            pool.memset(edges[:, NT:, :], 0.0).then_inc(matrices_zero, 1)
            pool.wait_ge(npass_set, 1)
            npass = pool.value_load(npass_i[0:1, 0:1], min_val=1, max_val=NWIN)
            with pool.Fori(0, npass) as j:
                with pool.Fori(0, CH - SLOTS + 1, SLOTS) as c:
                    for b in range(SLOTS):
                        pool.wait_ge(plain_ready, j * CH + c + b + 1)
                        pool.tensor_tensor(lo_hot[:, b, 2, 0:TN], lo_hot[:, b, 3, 0:TN],
                                           w_part[:, 2, bass.ds(c + b, 1)].to_broadcast([TN, TN]),
                                           ALU.mult).then_inc(part2_ready, 1)
            pool.wait_ge(edges_done, 1)
            pool.tensor_tensor(deg_sum_rows, counts[:, 0, 0:N], counts[:, 1, 0:N], ALU.add).then_inc(deg_rows, 1)
            for s in range(2, NT):
                pool.wait_ge(deg_rows, s - 1)
                pool.tensor_tensor(deg_sum_rows, deg_sum_rows, counts[:, s, 0:N], ALU.add).then_inc(deg_rows, 1)
            pool.wait_ge(rmax, KD)
            pool.wait_ge(dis_row, 1)
            pool.partition_all_reduce(inv_row, rs_row, 128, bass.bass_isa.ReduceOp.absmax).then_inc(rmax_all, 1)

            pool.wait_ge(ld_bdec, 16)
            pool.wait_ge(rscale, 2)
            for t in range(NT):
                for i, (t0, _) in enumerate(X_PARTS):
                    if t == t0:
                        pool.wait_ge(ld_X[i], 16)
                pool.tensor_tensor(X[:, t, :], X[:, t, :], bdec_row, ALU.add).then_inc(xb_ready, 1)
                if t < KD:
                    pool.wait_ge(ld_raw2[t % 2], 16 * (t // 2 + 1))
                    pool.tensor_tensor(raw2[t % 2], raw2[t % 2], inv_row, ALU.mult).then_inc(rmul, 1)
            with pool.Fori(0, NT) as t:
                pool.wait_ge(g0_out, t + 1)
                xt = X[:, bass.ds(t, 1), 0:H].rearrange("p a d -> p (a d)")
                pool.tensor_tensor(xt, xt, tile_of(gA, t), ALU.add).then_inc(g0_added, 1)
            with pool.Fori(0, NT) as t:
                pool.wait_ge(g_out, (STEPS - 1) * NT + t + 1)
                xt = X[:, bass.ds(t, 1), H:D].rearrange("p a d -> p (a d)")
                pool.tensor_tensor(xt, xt, tile_of(gA, t), ALU.add).then_inc(x3_ready, 1)
            with pool.Fori(0, PAIRS) as c:
                for d in range(KD):
                    pool.wait_ge(k_relu, c * KD + d + 1)
                    pool.tensor_tensor(kact[:, d, :], kact[:, d, :], kact[:, d, :], ALU.mult).then_inc(k_sq, 1)

        @block.vector
        def _(dve):
            def stats(xt, n):
                dve.bn_stats(st[0:TN, 0:6], xt[:, 0:HALF]).then_inc(ln_step, 1)
                dve.bn_stats(st[0:TN, 6:12], xt[:, HALF:D]).then_inc(ln_step, 1)
                dve.wait_ge(ln_step, n * 3 + 2)
                dve.bn_aggr(mv[0:TN, :], st[0:TN, :]).then_inc(ln_var, 1)
                dve.wait_ge(ln_std, n + 1)
                dve.reciprocal(rstd[0:TN, :], std[0:TN, :]).then_inc(ln_step, 1)
                dve.wait_ge(ln_step, n * 3 + 3)

            def normalise(dst_ap, xt):
                dve.tensor_scalar(dst_ap, xt, mv[0:TN, 0:1], rstd[0:TN, :],
                                  ALU.subtract, ALU.mult).then_inc(ln_out, 1)

            dve.wait_ge(consts, 8)
            count = [0]

            def then(ins):
                count[0] += 1
                ins.then_inc(prep, 1)
                dve.wait_ge(prep, count[0])

            dve.wait_ge(ld_edges, 48)
            then(dve.tensor_copy(e_f, e_int))
            then(dve.tensor_copy(extremes[:, 0, :], e_f[:, 1, :]))
            then(dve.tensor_scalar(extremes[:, 1, :], e_f[:, 1, :], -1.0, None, ALU.mult))
            then(dve.tensor_scalar(s0, e_f[:, 0, :], 1.0 / TN, 0.5 / TN - 0.5, ALU.mult, ALU.add))
            then(dve.tensor_scalar(s1, s0, MAGIC, None, ALU.add))
            then(dve.tensor_scalar(s2, s1, -MAGIC, None, ALU.add))
            then(dve.scalar_tensor_tensor(src_lo, s2, -float(TN), e_f[:, 0, :], ALU.mult, ALU.add))
            then(dve.tensor_scalar(key0, s2, float(W), 1.0, ALU.mult, ALU.add))
            rest = e_w
            for p in range(3):
                then(dve.tensor_copy(as_bf16, rest))
                then(dve.tensor_copy(w_part[:, p, :], as_bf16))
                if p < 2:
                    left = [s0, s1][p]
                    then(dve.tensor_tensor(left, rest, w_part[:, p, :], ALU.subtract))
                    rest = left
            for t in range(NT):
                b = t % 2
                dve.wait_ge(ld_x[b], 16 * (t // 2 + 1))
                stats(xin[b], t)
                if t >= 2:
                    dve.wait_ge(turned, 2 * t - 2)
                normalise(y[b], xin[b])

            dve.wait_ge(prep_max, 1)
            then(dve.tensor_tensor(s0, reduced[:, 0, :], reduced[:, 1, :], ALU.add))
            then(dve.tensor_reduce(flag[0:TN, 0:1], s0, AX.X, ALU.max))
            then(dve.tensor_scalar(flag[0:TN, 1:2], flag[0:TN, 0:1], W - 0.5, None, ALU.is_lt))
            then(dve.tensor_scalar(flag[0:TN, 2:3], flag[0:TN, 1:2], -float(NWIN - 1), float(NWIN),
                                   ALU.mult, ALU.add))
            dve.tensor_copy(npass_i[0:TN, :], flag[0:TN, 2:3]).then_inc(npass_set, 1)
            then(dve.tensor_scalar(s1, reduced[:, 1, :], -1.0, flag[0:TN, 1:2], ALU.mult, ALU.mult))
            then(dve.tensor_scalar(flag[0:TN, 3:4], flag[0:TN, 1:2], -1.0, 1.0, ALU.mult, ALU.add))
            dve.wait_ge(npass_set, 1)
            npass = dve.value_load(npass_i[0:1, 0:1], min_val=1, max_val=NWIN)

            def hots(c, b):
                dve.tensor_scalar(lo_hot[:, b, 3, 0:TN], iota[0:TN, 0:TN], src_lo[:, bass.ds(c, 1)], None,
                                  ALU.is_equal).then_inc(plain_ready, 1)
                dve.tensor_scalar(win_hot[:, b, :], iota[0:TN, :], key[:, bass.ds(c, 1)], None,
                                  ALU.is_equal).then_inc(hot_ready, 1)

            def add_chunk(c, b, i):
                start = dve.value_load(base_i[0:1, bass.ds(c, 1)], min_val=0, max_val=N - 1)
                dve.wait_ge(chunk_sum, i + 1)
                dve.wait_ge(chunk_added, i)
                window = edges[:, :, bass.ds(start, W)]
                dve.tensor_tensor(window, bank(4 + b, 2 * NT * W).rearrange("p (a w) -> p a w", w=W),
                                  window, ALU.add).then_inc(chunk_added, 1)

            dve.wait_ge(turned, 2 * NT)
            dve.wait_ge(matrices_zero, 2)
            with dve.Fori(0, npass) as j:
                in_pass = [0]

                def step(ins):
                    in_pass[0] += 1
                    ins.then_inc(window_set, 1)
                    dve.wait_ge(window_set, j * 9 + in_pass[0])

                step(dve.tensor_scalar(flag[0:TN, 0:1], win_start[0:TN, bass.ds(j, 1)], flag[0:TN, 3:4], None,
                                       ALU.mult))
                step(dve.tensor_scalar(s2, s1, flag[0:TN, 0:1], None, ALU.add))
                step(dve.tensor_copy(base_i, s2))
                step(dve.tensor_tensor(s0, e_f[:, 1, :], s2, ALU.subtract))
                step(dve.tensor_scalar(s2, s0, -0.5, None, ALU.is_gt))
                step(dve.scalar_tensor_tensor(s2, s0, W - 0.5, s2, ALU.is_lt, ALU.mult))
                step(dve.tensor_tensor(s0, s0, key0, ALU.add))
                step(dve.tensor_tensor(s0, s0, s2, ALU.mult))
                step(dve.tensor_scalar(key, s0, -1.0, None, ALU.add))
                for c in range(SLOTS - 1):
                    hots(c, c)
                hots(SLOTS - 1, SLOTS - 1)
                add_chunk(0, 0, j * CH)
                with dve.Fori(SLOTS, CH - SLOTS + 1, SLOTS) as c:
                    for b in range(SLOTS):
                        hots(c + b, b)
                        add_chunk(c + b - SLOTS + 1, (b + 1) % SLOTS, j * CH + c + b - SLOTS + 1)
                for c in range(CH - SLOTS + 1, CH):
                    add_chunk(c, c % SLOTS, j * CH + c)
            dve.wait_ge(chunk_added, npass * CH)
            dve.memset(flag[0:TN, 0:1], 0.0).then_inc(edges_done, 1)

            for k in range(KD):
                dve.wait_ge(rabs, k + 1)
                if k == 0:
                    dve.tensor_copy(rs_row, raw1[0]).then_inc(rmax, 1)
                else:
                    dve.wait_ge(rmax, k)
                    dve.tensor_tensor(rs_row, raw1[k % 2], rs_row, ALU.max).then_inc(rmax, 1)

            dve.wait_ge(deg_sum, 1)
            dve.tensor_scalar(deg_c[0:TN, :], bank(4, NT), 1.0, None, ALU.max).then_inc(deg_col, 1)
            dve.wait_ge(deg_root, 1)
            dve.reciprocal(dis_c[0:TN, :], deg_c[0:TN, :]).then_inc(dis_set, 1)
            dve.wait_ge(dis_set, 1)
            for t in range(NT):
                dve.tensor_scalar(dis_diags[:, t, :], ident[0:TN, 0:TN], dis_c[0:TN, t:t + 1], None,
                                  ALU.mult).then_inc(dis_diag, 1)
            dve.wait_ge(dis_row, 1)
            for g, (t0, k) in enumerate(GROUPS):
                with dve.Fori(0, NT) as s:
                    part = counts[:, bass.ds(s, 1), t0 * TN:(t0 + k) * TN].rearrange("p a n -> p (a n)")
                    dve.scalar_tensor_tensor(part, part, dis_c[0:TN, bass.ds(s, 1)], bank(5 + g, k * TN),
                                             ALU.mult, ALU.mult).then_inc(norm_set, 1)


            dve.wait_ge(rmax_all, 1)
            dve.tensor_scalar(rs_row, inv_row, 1e-12, 1.0 / 127.0, ALU.max, ALU.mult).then_inc(rscale, 1)
            dve.wait_ge(rscale, 1)
            dve.reciprocal(inv_row, rs_row).then_inc(rscale, 1)

            def round_rhs(k):
                dve.wait_ge(rmul, k + 1)
                dve.tensor_scalar(raw2[k % 2], raw2[k % 2], MAGIC, None, ALU.add).then_inc(rround, 1)
                dve.wait_ge(rround, k + 1)
                dve.tensor_scalar(qR[:, k, :], raw2[k % 2], -MAGIC, None, ALU.add).then_inc(rq, 1)

            for t in range(NT):
                xt = X[:, t, :]
                dve.wait_ge(xb_ready, t + 1)
                for h in range(2):
                    dve.wait_ge(dec_mm, 2 * t + h + 1)
                    xh = xt[:, h * HALF:(h + 1) * HALF]
                    dve.tensor_tensor(xh, bank(2 * (t % 2) + h), xh, ALU.add).then_inc(dec_out, 1)
                dve.wait_ge(dec_out, 2 * t + 2)
                stats(xt, t + NT)
                dve.wait_ge(q_step, 6 * t)
                normalise(y[0], xt)
                dve.wait_ge(ln_out, t + NT + 1)
                dve.tensor_reduce(amax[0:TN, :], y[0], AX.X, ALU.max,
                                  apply_absolute_value=True).then_inc(q_step, 1)
                dve.wait_ge(q_step, 6 * t + 1)
                dve.tensor_scalar(qscale[0:TN, :], amax[0:TN, :], 1e-12, 1.0 / 127.0, ALU.max, ALU.mult).then_inc(q_step, 1)
                dve.wait_ge(q_step, 6 * t + 2)
                dve.reciprocal(linv[0:TN, :], qscale[0:TN, :]).then_inc(q_step, 1)
                dve.tensor_copy(lscale[0:TN, t:t + 1], qscale[0:TN, :]).then_inc(q_step, 1)
                dve.wait_ge(q_step, 6 * t + 4)
                dve.tensor_scalar(y[0], y[0], linv[0:TN, :], MAGIC, ALU.mult, ALU.add).then_inc(q_step, 1)
                dve.wait_ge(q_step, 6 * t + 5)
                dve.wait_ge(q_turned, t)
                dve.tensor_scalar(qtile, y[0], -MAGIC, None, ALU.add).then_inc(q_step, 1)
                if t < KD:
                    round_rhs(t)

            def dot_products(gt, k, t):
                for i, (dot, junk) in enumerate(((dot_a, tmp[0]), (dot_b, tmp[1]))):
                    dve.tensor_tensor_reduce(junk, gt, wg_row[k % 2][:, i * H:(i + 1) * H], 1.0, 0.0,
                                             ALU.mult, ALU.add, dot[0:TN, t:t + 1]).then_inc(dots, 1)

            def integer_tile(t):
                if t > 2:
                    dve.wait_ge(dots, 2 * t - 4)
                for h in range(2):
                    dve.wait_ge(int_mm, 2 * t + h + 1)
                    if t:
                        dve.wait_ge(x2_ready, 2 * t + h - 1)
                    dve.scalar_tensor_tensor(tmp[h], bank(h), lscale[0:TN, t:t + 1],
                                             rs_row[0:TN, h * HALF:(h + 1) * HALF], ALU.mult,
                                             ALU.mult).then_inc(int_scaled, 1)
                    dve.wait_ge(int_scaled, 2 * t + h + 1)
                    xh = X[:, t, h * HALF:(h + 1) * HALF]
                    dve.tensor_tensor(xh, xh, tmp[h], ALU.add).then_inc(x2_ready, 1)
                dve.wait_ge(x2_ready, 2 * t + 2)
                stats(X[:, t, :], t + 2 * NT)
                dve.wait_ge(turned, 2 * NT + 2 * t)
                normalise(y[1], X[:, t, :])

            def graph_input(t):
                dve.wait_ge(g0_mm, t + 1)
                dve.tensor_tensor(gA[:, t, :], bank(4), b1_row, ALU.add).then_inc(g0_out, 1)
                dve.wait_ge(g0_out, t + 1)
                dve.wait_ge(x2_ready, 2 * min(t + 3, NT))
                dve.wait_ge(dots, 2 * t)
                dot_products(gA[:, t, :], 0, t)

            dve.wait_ge(ld_wg[0], 16)
            dve.wait_ge(ld_b1, 16)
            dve.wait_ge(q_step, 6 * NT)
            integer_tile(0)
            integer_tile(1)
            for t in range(2, NT):
                integer_tile(t)
                graph_input(t - 2)
            graph_input(NT - 2)
            graph_input(NT - 1)

            dve.wait_ge(ld_small, 48)
            for k in range(STEPS):
                g_in, g_next = (gA, gB) if k % 2 == 0 else (gB, gA)

                def matrix_parts(g):
                    t0, cnt = GROUPS[g]
                    with dve.Fori(0, NT) as s:
                        dve.wait_ge(tanh_out, s + (k * len(GROUPS) + g) * NT + 1)
                        m = mring[:, bass.ds(s, 1), 0:cnt * TN].rearrange("p a n -> p (a n)")
                        c = counts[:, bass.ds(s, 1), t0 * TN:(t0 + cnt) * TN].rearrange("p a n -> p (a n)")
                        dve.tensor_tensor(m, m, c, ALU.mult).then_inc(m_set, 1)

                def new_state(g):
                    t0, cnt = GROUPS[g]
                    for t in range(t0, t0 + cnt):
                        if t < t0 + cnt - 1:
                            dve.wait_ge(g_mm, k * (NT - len(GROUPS)) + t - g + 1)
                        else:
                            dve.wait_ge(slot_free, (k * len(GROUPS) + g + 1) * NT)
                        dve.tensor_tensor(g_next[:, t, :], bank(t % 5), g_in[:, t, :], ALU.add).then_inc(g_out, 1)
                    if k + 1 < STEPS:
                        for t in range(t0, t0 + cnt):
                            dve.wait_ge(g_out, k * NT + t + 1)
                            dve.wait_ge(dots, 2 * ((k + 1) * NT + t))
                            dot_products(g_next[:, t, :], k + 1, t)

                dve.wait_ge(dots, 2 * NT * (k + 1))
                dve.tensor_scalar(bias_b[0:TN, :], dot_b[0:TN, :], bg_row[0:TN, k:k + 1], None,
                                  ALU.add).then_inc(bias_set, 1)
                with dve.Fori(0, NT) as t:
                    dve.tensor_scalar(tile_of(diag, t), ident[0:TN, 0:TN], dot_a[0:TN, bass.ds(t, 1)], None,
                                      ALU.mult).then_inc(diag_set, 1)
                matrix_parts(0)
                matrix_parts(1)
                if k + 1 < STEPS:
                    dve.wait_ge(ld_wg[(k + 1) % 2], 16 * ((k + 1) // 2 + 1))
                if k == 1:
                    dve.wait_ge(g0_added, NT)
                new_state(0)
                matrix_parts(2)
                new_state(1)
                new_state(2)

            dve.wait_ge(x3_ready, NT)
            dve.tensor_scalar(mu[:, 2:4, :], mu[:, 0:2, :], -1.0, 1.0, ALU.mult, ALU.add).then_inc(mu_set, 1)
            dve.memset(last_col, 0.0).then_inc(last_kept, 1)

            def pair_norm(c):
                for b in range(2):
                    xt = X[:, 2 * c + b, :]
                    stats(xt, 2 * c + b + 3 * NT)
                    dve.wait_ge(pair_turned, 4 * c)
                    normalise(yl[b], xt)

            def pair_mix(c):
                for i, (mixed, ready) in enumerate(((xkT, mix_k), (xrT, mix_r))):
                    if i == 0:
                        dve.wait_ge(k_mm, KD * c)
                    else:
                        dve.wait_ge(r_mm, 4 * c)
                    for k in range(KD):
                        dve.wait_ge(part_mix, 2 * KD * c + i * KD + k + 1)
                        dve.scalar_tensor_tensor(mixed[:, k, :], xl[:, k, 1:PN + 1], mu[:, i, k:k + 1],
                                                 mixt[k % 2], ALU.mult, ALU.add).then_inc(ready, 1)

            def pair_out(c):
                for b in range(2):
                    for h in range(2):
                        n = 4 * c + 2 * b + h
                        dve.wait_ge(v_mm, n + 1)
                        dve.wait_ge(r_out, n + 1)
                        dve.wait_ge(y_out, 4 * c + max(2 * b + h - 1, 0))
                        dve.tensor_tensor(prod[h], bank(6 + h), gate[b][:, h * HALF:(h + 1) * HALF],
                                          ALU.mult).then_inc(v_prod, 1)
                        dve.wait_ge(v_prod, n + 1)
                        xh = X[:, 2 * c + b, h * HALF:(h + 1) * HALF]
                        dve.tensor_tensor(xh, xh, prod[h], ALU.add).then_inc(y_out, 1)

            pair_norm(0)
            pair_mix(0)
            for c in range(PAIRS - 1):
                pair_norm(c + 1)
                pair_mix(c + 1)
                pair_out(c)
            pair_out(PAIRS - 1)

        @block.scalar
        def _(act):
            def root(n):
                act.wait_ge(ln_var, n + 1)
                act.activation(std[0:TN, :], mv[0:TN, 1:2], ACT.Sqrt, bias=eps[0:TN, :]).then_inc(ln_std, 1)

            act.wait_ge(consts, 8)
            for t in range(NT):
                root(t)
                for half in range(2):
                    act.wait_ge(turned, 2 * t + half + 1)
                    act.activation(xlnT[:, 4 * half:4 * half + 4, t * TN:(t + 1) * TN],
                                   bank(2 * (t % 2) + half, 4 * TN, 128).rearrange("p (k n) -> p k n", k=4),
                                   ACT.Copy).then_inc(turned_out, 1)

            def weigh(c, b, i):
                act.wait_ge(plain_ready, i + 1)
                for p in range(2):
                    last = act.activation(lo_hot[:, b, p, 0:TN], lo_hot[:, b, 3, 0:TN], ACT.Copy,
                                          scale=w_part[:, p, bass.ds(c, 1)])
                last.then_inc(part01_ready, 1)

            def group_out(n):
                act.wait_ge(mm, n + 1)
                if n < 12:
                    c0, cn = COLS[n // MB]
                    m = n % MB
                    act.activation(hT[:, m, c0:c0 + cn], bank(n % 4, cn), ACT.Sigmoid,
                                   bias=benc_c[0:TN, m:m + 1]).then_inc(mm_out, 1)
                else:
                    act.activation(h2[:, n - 12, :], bank(n % 4, EMB), ACT.Copy).then_inc(mm_out, 1)

            act.wait_ge(ld_enc, 32)
            n = 0
            for c in range(CH):
                weigh(c, c % SLOTS, c)
                while n < 12 + NT and group_end(n) * CH <= (c - 2) * DENSE:
                    group_out(n)
                    n += 1
            while n < 12 + NT:
                group_out(n)
                n += 1
            act.wait_ge(npass_set, 1)
            npass = act.value_load(npass_i[0:1, 0:1], min_val=1, max_val=NWIN)
            with act.If(npass > 1):
                with act.Fori(1, npass) as j:
                    with act.Fori(0, CH - SLOTS + 1, SLOTS) as c:
                        for b in range(SLOTS):
                            weigh(c + b, b, j * CH + c + b)
            for m in range(MB):
                if m == 1:
                    act.wait_ge(deg_col, 1)
                    act.activation(deg_c[0:TN, :], deg_c[0:TN, :], ACT.Sqrt).then_inc(deg_root, 1)
                for i, (c0, cn) in enumerate(COLS):
                    if m == 0:
                        for k in range(3 * i, min(3 * i + 3, KD)):
                            act.wait_ge(ld_raw1[k % 2], 16 * (k // 2 + 1))
                            act.activation(raw1[k % 2], raw1[k % 2], ACT.Abs).then_inc(rabs, 1)
                    act.wait_ge(mm, n + 1)
                    act.activation(houtT[:, m, c0:c0 + cn], bank(n % 4, cn), ACT.Copy).then_inc(mm_out, 1)
                    n += 1

            def q_copy(t):
                act.wait_ge(q_turned, t + 1)
                turned_q = ps[:, 4, :].bitcast(BF16)[:, 0:KD * 126].rearrange("p (k n) -> p k n", k=KD)
                act.activation(qT[:, bass.ds(t, 1), :, :].rearrange("p t k n -> p (t k) n"),
                               turned_q[:, :, 0:TN], ACT.Copy).then_inc(q_copied, 1)

            root(NT)
            with act.Fori(0, NT - 1) as t:
                root(t + NT + 1)
                q_copy(t)
            q_copy(NT - 1)

            def x_copy(t):
                for half in range(2):
                    act.wait_ge(g0_mm, t)
                    act.wait_ge(turned, 2 * NT + 2 * t + half + 1)
                    act.activation(xT[:, 4 * half:4 * half + 4, :],
                                   bank(2 + half, 4 * TN, 128).rearrange("p (k n) -> p k n", k=4),
                                   ACT.Copy).then_inc(turned_out, 1)

            act.wait_ge(rq, KD)
            root(2 * NT)
            with act.Fori(0, NT - 1) as t:
                root(t + 2 * NT + 1)
                x_copy(t)
            x_copy(NT - 1)

            with act.Fori(0, STEPS) as k:
                act.wait_ge(bias_set, k + 1)
                act.wait_ge(a_row, k + 1)
                for g, (t0, cnt) in enumerate(GROUPS):
                    with act.Fori(0, NT) as s:
                        if g == 0:
                            act.wait_ge(slot_free, k * (len(GROUPS) * NT))
                        else:
                            act.wait_ge(slot_free, k * (len(GROUPS) * NT) + (g - 1) * NT + s + 1)
                        m = mring[:, bass.ds(s, 1), 0:cnt * TN].rearrange("p a n -> p (a n)")
                        act.activation(m, bank(5 + g, cnt * TN), ACT.Tanh,
                                       bias=bias_b[0:TN, bass.ds(s, 1)]).then_inc(tanh_out, 1)

            def pair_copy(c):
                for b in range(2):
                    for half in range(2):
                        act.wait_ge(pair_turned, 4 * c + 2 * b + half + 1)
                        act.activation(xl[:, 4 * half:4 * half + 4, 1 + b * TN:1 + (b + 1) * TN],
                                       bank(2 * b + half, 4 * TN, 128).rearrange("p (k n) -> p k n", k=4),
                                       ACT.Copy).then_inc(pair_copied, 1)
                act.wait_ge(last_kept, c + 1)
                act.activation(xl[:, :, 0], last_col, ACT.Copy).then_inc(col_set, 1)

            def mix_terms(c):
                act.wait_ge(pair_copied, 4 * c + 4)
                act.wait_ge(col_set, c + 1)
                for i, ready in enumerate((mix_k, mix_r)):
                    for k in range(KD):
                        if k >= 2:
                            act.wait_ge(ready, KD * c + k - 1)
                        elif i == 1:
                            act.wait_ge(mix_k, KD * c + KD)
                        else:
                            act.wait_ge(mix_r, KD * c)
                        act.activation(mixt[k % 2], xl[:, k, 0:PN], ACT.Copy,
                                       scale=mu[:, 2 + i, k:k + 1]).then_inc(part_mix, 1)
                act.wait_ge(mix_r, KD * c + KD)
                act.activation(last_col, xl[:, :, PN], ACT.Copy).then_inc(last_kept, 1)

            def pair_out(c):
                act.wait_ge(v_mm, 4 * c)
                for d in range(KD):
                    act.wait_ge(k_mm, KD * c + d + 1)
                    act.activation(kact[:, d, :], bank(d % 4, PN, 128), ACT.Relu).then_inc(k_relu, 1)
                act.wait_ge(v_prod, 4 * c)
                for b in range(2):
                    for h in range(2):
                        act.wait_ge(r_mm, 4 * c + 2 * b + h + 1)
                        act.activation(gate[b][:, h * HALF:(h + 1) * HALF], bank(4 + h),
                                       ACT.Sigmoid).then_inc(r_out, 1)

            for b in range(2):
                root(3 * NT + b)
            act.wait_ge(mu_set, 1)
            pair_copy(0)
            mix_terms(0)
            with act.Fori(0, PAIRS - 1) as c:
                for b in range(2):
                    root(3 * NT + 2 * c + 2 + b)
                pair_out(c)
                pair_copy(c + 1)
                mix_terms(c + 1)
            pair_out(PAIRS - 1)

        @block.tensor
        def _(pe):
            def turn(tile, banks, done):
                for half in range(2):
                    for k in range(4):
                        f = 4 * half + k
                        t = pe.transpose(bank(banks[half], TN, 128, k * TN), tile[:, f * 128:(f + 1) * 128],
                                         ident[0:TN, 0:TN])
                    t.then_inc(done, 1)

            pe.wait_ge(consts, 8)
            for t in range(NT):
                b = t % 2
                pe.wait_ge(ln_out, t + 1)
                if t >= 2:
                    pe.wait_ge(turned_out, 2 * t - 2)
                turn(y[b], (2 * b, 2 * b + 1), turned)

            def chunk_product(b, i):
                pe.wait_ge(part01_ready, i + 1)
                pe.wait_ge(part2_ready, i + 1)
                pe.wait_ge(hot_ready, i + 1)
                for p in range(3):
                    pe.matmul(bank(4 + b, NT * W), lo_hot[:, b, p, 0:TN], win_hot[:, b, :],
                              start=(p == 0), stop=(p == 2), skip_group_check=True)
                pe.matmul(bank(4 + b, NT * W, TN, NT * W), lo_hot[:, b, 3, 0:TN], win_hot[:, b, :],
                          start=False, stop=True, skip_group_check=True).then_inc(chunk_sum, 1)

            def dense_product(i):
                if i < 12 * KD:
                    n, k = divmod(i, KD)
                    c0, cn = COLS[n // MB]
                    m = n % MB
                    if i == 0:
                        pe.wait_ge(ld_enc, 32)
                        pe.wait_ge(turned_out, 2 * NT)
                    if k == 0 and n >= 4:
                        pe.wait_ge(mm_out, n - 3)
                    last = pe.matmul(bank(n % 4, cn), wenc[:, k, m * TN:(m + 1) * TN],
                                     xlnT[:, k, c0:c0 + cn], start=(k == 0), stop=(k == KD - 1))
                    if k == KD - 1:
                        last.then_inc(mm, 1)
                else:
                    t, k = divmod(i - 12 * KD, MB)
                    n = 12 + t
                    if t == 0 and k == 0:
                        pe.wait_ge(ld_conv, 16)
                        pe.wait_ge(mm_out, 12)
                    elif k == 0:
                        pe.wait_ge(mm_out, n - 3)
                    last = pe.matmul(bank(n % 4, EMB), hT[:, k, t * TN:(t + 1) * TN], convw[:, k, :],
                                     start=(k == 0), stop=(k == MB - 1))
                    if k == MB - 1:
                        last.then_inc(mm, 1)

            for c in range(CH):
                if c >= SLOTS:
                    pe.wait_ge(chunk_added, c - SLOTS + 1)
                chunk_product(c % SLOTS, c)
                for i in range(c * DENSE // CH, (c + 1) * DENSE // CH):
                    dense_product(i)
            pe.wait_ge(npass_set, 1)
            npass = pe.value_load(npass_i[0:1, 0:1], min_val=1, max_val=NWIN)
            with pe.If(npass > 1):
                with pe.Fori(1, npass) as j:
                    with pe.Fori(0, CH - SLOTS + 1, SLOTS) as c:
                        for b in range(SLOTS):
                            pe.wait_ge(chunk_added, j * CH + c + b - SLOTS + 1)
                            chunk_product(b, j * CH + c + b)

            def degrees():
                pe.wait_ge(deg_rows, NT - 1)
                for t in range(NT):
                    last = pe.matmul(bank(4, 1, TN, t), deg_sum_rows[:, t * TN:(t + 1) * TN], ones[0:TN, 0:1],
                                     start=True, stop=True, skip_group_check=True)
                last.then_inc(deg_sum, 1)

            def root_rows():
                pe.wait_ge(dis_diag, NT)
                for t in range(NT):
                    last = pe.matmul(bank(5 + t // 4, TN, TN, (t % 4) * TN), ones[0:TN, 0:TN],
                                     dis_diags[:, t, :], start=True, stop=True, skip_group_check=True)
                last.then_inc(dis_row, 1)

            pe.wait_ge(edges_done, 1)
            n = 12 + NT
            pe.wait_ge(mm_out, n)
            for m in range(MB):
                for i, (c0, cn) in enumerate(COLS):
                    pe.wait_ge(mm_out, n - 3)
                    for s in range(NT):
                        pe.matmul(bank(n % 4, cn), h2[:, s, m * TN:(m + 1) * TN],
                                  edges[:, s, c0:c0 + cn], start=(s == 0), stop=False)
                    if n == 12 + NT:
                        pe.wait_ge(ld_lin, 16)
                    for k in range(MB):
                        last = pe.matmul(bank(n % 4, cn), linw[:, k, m * TN:(m + 1) * TN], hT[:, k, c0:c0 + cn],
                                         start=False, stop=(k == MB - 1))
                    last.then_inc(mm, 1)
                    n += 1
                    if (m, i) == (1, 0):
                        degrees()
                    if (m, i) == (1, 2):
                        root_rows()

            def turn_q(t):
                pe.wait_ge(q_step, 6 * t + 6)
                if t:
                    pe.wait_ge(q_copied, t)
                for f in range(KD):
                    last = pe.transpose(ps[:, 4, :].bitcast(BF16)[:, f * 126:f * 126 + TN],
                                        qtile[:, f * 128:(f + 1) * 128], identb[0:TN, 0:TN])
                last.then_inc(q_turned, 1)

            pe.wait_ge(ld_dec, 16)
            pe.wait_ge(mm_out, NG)
            for t in range(NT):
                for h in range(2):
                    if t >= 2:
                        pe.wait_ge(dec_out, 2 * (t - 2) + h + 1)
                    for k in range(MB):
                        last = pe.matmul(bank(2 * (t % 2) + h), houtT[:, k, t * TN:(t + 1) * TN],
                                         wdec[:, k, h * HALF:(h + 1) * HALF], start=(k == 0), stop=(k == MB - 1))
                    last.then_inc(dec_mm, 1)
                if t:
                    turn_q(t - 1)
            turn_q(NT - 1)

            def integer_product(t):
                pe.wait_ge(q_copied, t + 1)
                pe.wait_ge(int_scaled, 2 * t)
                for h in range(2):
                    for k in range(KD):
                        lhs = qT[:, bass.ds(t, 1), k, :].rearrange("p t n -> p (t n)")
                        last = pe.matmul(bank(h), lhs, qR[:, k, h * HALF:(h + 1) * HALF],
                                         start=(k == 0), stop=(k == KD - 1))
                    last.then_inc(int_mm, 1)

            def graph_input(t):
                pe.wait_ge(turned_out, 2 * NT + 2 * t + 2)
                pe.wait_ge(g0_out, t)
                for k in range(KD):
                    last = pe.matmul(bank(4), xT[:, k, :], w1[:, k, :], start=(k == 0), stop=(k == KD - 1))
                last.then_inc(g0_mm, 1)

            def turn_x(t):
                pe.wait_ge(ln_out, 2 * NT + t + 1)
                pe.wait_ge(turned_out, 2 * NT + 2 * t)
                turn(y[1], (2, 3), turned)

            pe.wait_ge(rq, KD)
            pe.wait_ge(dec_out, 2 * NT)
            integer_product(0)
            integer_product(1)
            turn_x(0)
            pe.wait_ge(ld_w1, 16)
            with pe.Fori(2, NT) as t:
                integer_product(t)
                graph_input(t - 2)
                turn_x(t - 1)
            graph_input(NT - 2)
            turn_x(NT - 1)
            graph_input(NT - 1)

            pe.wait_ge(g0_out, NT)
            with pe.Fori(0, STEPS, 2) as k2:
                for i in range(2):
                    k = k2 + i
                    g_in = (gA, gB)[i]
                    pe.wait_ge(diag_set, k * NT + NT)
                    pe.wait_ge(tanh_out, k * (len(GROUPS) * NT))
                    for t in range(NT):
                        last = pe.matmul(bank(5 + t // 4, TN, TN, (t % 4) * TN), ones[0:TN, 0:TN], diag[:, t, :],
                                         start=True, stop=True, skip_group_check=True)
                    last.then_inc(a_row, 1)
                    for g, (t0, cnt) in enumerate(GROUPS):
                        for s in range(NT):
                            pe.wait_ge(m_set, k * (len(GROUPS) * NT) + g * NT + s + 1)
                            for d in range(cnt):
                                t = t0 + d
                                if s == 0 and t >= 5:
                                    pe.wait_ge(g_out, k * NT + t - 4)
                                last = pe.matmul(bank(t % 5), mring[:, s, d * TN:(d + 1) * TN], g_in[:, s, :],
                                                 start=(s == 0), stop=(s == NT - 1))
                                if s == NT - 1 and d < cnt - 1:
                                    last.then_inc(g_mm, 1)
                            last.then_inc(slot_free, 1)

            def turn_pair(c):
                for b in range(2):
                    pe.wait_ge(ln_out, 2 * c + 3 * NT + b + 1)
                    turn(yl[b], (2 * b, 2 * b + 1), pair_turned)

            def pair_products(c, more):
                pe.wait_ge(pair_copied, 4 * c + 4)
                for d in range(KD):
                    if d >= 4:
                        pe.wait_ge(k_relu, KD * c + d - 3)
                    for k in range(KD):
                        if d == 0:
                            pe.wait_ge(mix_k, KD * c + k + 1)
                        last = pe.matmul(bank(d % 4, PN, 128), wk[k][:, d * 128:(d + 1) * 128], xkT[:, k, :],
                                         start=(k == 0), stop=(k == KD - 1))
                    last.then_inc(k_mm, 1)
                for b in range(2):
                    for h in range(2):
                        pe.wait_ge(r_out, 4 * c + max(2 * b + h - 1, 0))
                        for k in range(KD):
                            if b == 0 and h == 0:
                                pe.wait_ge(mix_r, KD * c + k + 1)
                            last = pe.matmul(bank(4 + h), xrT[:, k, b * TN:(b + 1) * TN],
                                             wr[:, k, h * HALF:(h + 1) * HALF], start=(k == 0), stop=(k == KD - 1))
                        last.then_inc(r_mm, 1)
                if more:
                    pe.wait_ge(k_relu, KD * c + KD)
                    turn_pair(c + 1)
                for b in range(2):
                    for h in range(2):
                        pe.wait_ge(v_prod, 4 * c + max(2 * b + h - 1, 0))
                        for d in range(KD):
                            if b == 0 and h == 0:
                                pe.wait_ge(k_sq, KD * c + d + 1)
                            last = pe.matmul(bank(6 + h), kact[:, d, b * TN:(b + 1) * TN],
                                             wv[:, d, h * HALF:(h + 1) * HALF], start=(d == 0), stop=(d == KD - 1))
                        last.then_inc(v_mm, 1)

            pe.wait_ge(g_out, STEPS * NT)
            turn_pair(0)
            pe.wait_ge(ld_wk, 16 * KD)
            pe.wait_ge(ld_wr, 16)
            pe.wait_ge(ld_wv, 16)
            with pe.Fori(0, PAIRS - 1) as c:
                pair_products(c, True)
            pair_products(PAIRS - 1, False)


def kernel(x, src, dst, edge_weight, L0_gnn_wenc, L0_gnn_benc, L0_gnn_wdec, L0_gnn_bdec, L0_gnn_conv_weight,
           L0_gnn_lin_weight, L0_ffn_rhs, L1_gnn_W1, L1_gnn_b1, L1_gnn_Wg, L1_gnn_bg, L1_ffn_W_r, L1_ffn_W_k,
           L1_ffn_W_v, L1_ffn_mu_r, L1_ffn_mu_k):
    import numpy as np
    import concourse.bacc as bacc
    from concourse.bass_utils import run_bass_kernel_spmd

    def chunks(a):
        return np.asarray(a).reshape(CH, TN).T

    def blocks(a, p):
        return np.asarray(a).reshape(-1, p).T

    arrays = {
        "x": x, "src": chunks(src), "dst": chunks(dst), "edge_w": chunks(edge_weight),
        "wenc_t": np.asarray(L0_gnn_wenc).T, "benc": blocks(L0_gnn_benc, TN),
        "wdec_t": np.asarray(L0_gnn_wdec).T, "bdec": L0_gnn_bdec,
        "conv": L0_gnn_conv_weight, "lin_t": np.asarray(L0_gnn_lin_weight).T, "rhs": L0_ffn_rhs,
        "W1": L1_gnn_W1, "b1": L1_gnn_b1, "Wg": np.asarray(L1_gnn_Wg).reshape(STEPS, 2 * H),
        "bg": np.asarray(L1_gnn_bg).reshape(STEPS),
        "Wr_t": np.asarray(L1_ffn_W_r).T, "Wk_t": np.asarray(L1_ffn_W_k).T, "Wv_t": np.asarray(L1_ffn_W_v).T,
        "mu_r": blocks(L1_ffn_mu_r, 128), "mu_k": blocks(L1_ffn_mu_k, 128),
    }
    arrays = {k: np.ascontiguousarray(v) for k, v in arrays.items()}
    nc = bacc.Bacc("TRN2", target_bir_lowering=False, num_devices=1)
    args = {k: nc.dram_tensor(f"in_{k}", v.shape, mybir.dt.from_np(v.dtype), kind="ExternalInput").ap()
            for k, v in arrays.items()}
    args["out"] = nc.dram_tensor("out_x", (N, D), F32, kind="ExternalOutput").ap()
    build(nc, **args)
    got = run_bass_kernel_spmd(nc, [{f"in_{k}": v for k, v in arrays.items()}], core_ids=[0])
    return got.results[0]["out_x"]
```

```python
from contextlib import ExitStack

import concourse.bass as bass
from concourse import mybir

F32 = mybir.dt.float32
BF16 = mybir.dt.bfloat16
F32R = mybir.dt.float32r
I32 = mybir.dt.int32
I16 = mybir.dt.int16
ALU = mybir.AluOpType
ACT = mybir.ActivationFunctionType
AX = mybir.AxisListType

N, D, E = 1250, 1024, 20000
TN = 125
NT = N // TN
CH = E // TN
EMB = 500
MB = EMB // TN
KD = D // 128
H = 512
STEPS = 4
W = 22
NWIN = -(-N // W)
PADN = 1275
HALF = 512
MAGIC = float(3 << 22)
EPS = 1e-5
COLS = [(0, 418), (418, 416), (834, 416)]
RING = 5
PARTS = 3 * NT
SLOTS = 4
DENSE = 3 * MB * KD + NT * MB
EARLY = 4
LN_AT = {t: 4 + 4 * (t - EARLY) for t in range(EARLY, NT)}
UNROLLED = 28
STAGED = 5
GROUPS = [(0, 4), (4, 4), (8, 2)]
HALVES = 2
HT = NT // HALVES
HN = HT * TN
BLOCKS = 3 * KD
HP = HN + 1
HGROUPS = [(0, 314), (314, 312)]
REAL = [(0, 314), (314, 311)]
OPERAND = [0, 1, 1, 0]
MIX_AT = {5: (0, 1, 2, 3), 6: (4, 5, 6), 7: (7,)}
STORES = [(0, 4), (4, 6), (6, 8)]
ARENA = 52360
SPLIT = 35744


def group_end(n):
    return KD * min(n + 1, 12) + MB * max(n + 1 - 12, 0)


def tiles_for(n):
    return -(-n // TN)


def build(nc, x, src, dst, edge_w, wenc_t, benc, wdec_t, bdec, conv, lin_t, rhs, W1, b1, Wg, bg,
          W_ffn, mu_r, mu_k, out):
    with ExitStack() as ctx:
        def sem(name):
            return ctx.enter_context(nc.semaphore(name))

        def sb(name, shape, dt=F32):
            return ctx.enter_context(nc.sbuf_tensor(name, shape, dt))

        arena_low = sb("arena_low", [128, SPLIT])
        arena_high = sb("arena_high", [128, ARENA - SPLIT])
        arena_base = nc.sbuf_base - 4 * ARENA

        def own(name, off, shape, dt=F32R):
            return nc.alloc_sbuf_tensor_at(name, shape, dt, offset=arena_base + 4 * off)

        def aligned(off):
            return -(-off // 8) * 8

        def at(off, n, rows=TN):
            if off + n <= SPLIT:
                return arena_low[0:rows, off:off + n]
            return arena_high[0:rows, off - SPLIT:off - SPLIT + n]

        def tiles(off, a, b, rows=TN):
            return at(off, a * b, rows).rearrange("p (a b) -> p a b", b=b)

        edges = tiles(0, 2 * NT, PADN)
        counts = edges[:, NT:2 * NT, :]
        X = tiles(0, NT, D)
        o_tail = NT * D
        assert PADN >= N + W
        raw2 = [at(o_tail + b * D, D, 128) for b in range(2)]
        xT = tiles(o_tail, KD, TN, 128)
        o_a = aligned(2 * NT * PADN)
        xlnT = tiles(o_a, KD, N, 128)
        h2 = tiles(o_a, NT, EMB)
        qT = at(o_a, NT * KD * TN // 2, 128).bitcast(BF16).rearrange("p (t k n) -> p t k n", t=NT, k=KD)
        counts16 = at(NT * PADN, NT * N // 2).bitcast(I16).rearrange("p (s n) -> p s n", n=N)
        x_staged = tiles(NT * PADN + NT * N // 2, STAGED, D)
        assert NT * PADN + NT * N // 2 + STAGED * D <= o_a
        g_lo = own("g_lo", NT * PADN + NT * N // 2, [128, NT, H])
        g_hi = own("g_hi", o_a, [128, NT, H])
        o_b = aligned(o_a + NT * H)
        houtT = tiles(o_b, MB, N)
        state = own("state", o_b, [128, NT, H], F32)[0:TN]
        o_c = aligned(o_b + NT * H)
        assert o_c == SPLIT
        wenc = tiles(o_c, KD, EMB, 128)
        wdec = tiles(o_c, MB, D)
        w1 = tiles(o_c, KD, H, 128)
        m_scratch = own("m_scratch", o_c, [128, RING, 4 * TN], F32)
        o_hi = aligned(o_c + RING * 4 * TN)
        o_lo = aligned(o_hi + RING * 4 * TN)
        m_hi = own("m_hi", o_hi, [128, RING, 4 * TN])
        m_lo = own("m_lo", o_lo, [128, RING, 4 * TN])
        diag = tiles(o_lo + RING * 4 * TN, NT, TN)
        o_d = o_c + KD * H
        hT = tiles(o_d, MB, N)
        qR = at(o_d, KD * D // 2, 128).bitcast(BF16).rearrange("p (k n) -> p k n", k=KD)
        o_e = aligned(o_d + NT * H)
        xin = [at(o_e + b * D, D) for b in range(2)]
        y = [at(o_e + (2 + b) * D, D) for b in range(2)]
        convw = tiles(o_e, MB, EMB)
        linw = tiles(o_e + 2 * D, MB, EMB)
        raw1 = [at(o_e + b * D, D, 128) for b in range(2)]
        qtile = [at(o_e + b * D // 2, D // 2).bitcast(BF16) for b in range(2)]
        b1_row = at(o_e, H)
        tmp = [at(o_e + D + b * H, H) for b in range(2)]
        o_f = aligned(o_e + 4 * D)
        bdec_row = at(o_f, D)
        rs_row = at(o_f + D, D, 128)
        inv_row = at(o_f + 2 * D, D, 128)
        wg_row = [at(o_f + b * D, D) for b in range(2)]
        deg_sum_rows = at(o_f + 2 * D, N)
        first_counts = at(o_f + 2 * D, N // 2).bitcast(I16)

        def columns(i, k=1):
            return at(o_f + i * CH, k * CH)

        e_int = columns(0, 2).bitcast(I32).rearrange("p (a c) -> p a c", a=2)
        e_f = columns(2, 2).rearrange("p (a c) -> p a c", a=2)
        e_w = columns(4)
        w_part = columns(5, 3).rearrange("p (a c) -> p a c", a=3)
        src_lo, s0, s1, s2, key0, key = (columns(8 + i) for i in range(6))
        base_i = columns(14).bitcast(I32)
        extremes = at(o_d, 2 * CH).rearrange("p (a c) -> p a c", a=2)
        reduced = at(o_d + 2 * CH, 2 * CH).rearrange("p (a c) -> p a c", a=2)
        as_bf16 = at(o_d + 4 * CH, CH // 2).bitcast(BF16)
        hot_words = 252 + NT * W // 2
        o_hot = [o_e + 3 * D, o_e + 3 * D + hot_words, o_f + 15 * CH, o_f + 15 * CH + hot_words]
        assert len(o_hot) == SLOTS and 2 * hot_words <= D and o_hot[3] + hot_words <= ARENA
        lo_hot = [at(o, 252).bitcast(BF16).rearrange("p (a s) -> p a s", a=4) for o in o_hot]
        win_hot = [at(o + 252, NT * W // 2).bitcast(BF16) for o in o_hot]

        w_raw = [own(f"w_raw{b}", o_tail + b * D, [128, D], F32) for b in range(2)]
        o_xop = [aligned(o_tail + 2 * D), o_a]
        x_hi = [own(f"x_hi{b}", o_xop[b], [128, KD, HP]) for b in range(2)]
        x_lo = [own(f"x_lo{b}", aligned(o_xop[b] + KD * HP), [128, KD, HP]) for b in range(2)]
        o_mixed = aligned(o_xop[0] + 2 * KD * HP)
        mixed = [at(o_mixed + b * HP, HP, 128) for b in range(2)]
        o_w = [aligned(NT * PADN + NT * N // 2 + NT * H), aligned(o_f + 2 * D + 2 * HN - D)]
        w_hi = [own(f"w_hi{b}", aligned(o_e + 2 * D) + b * D, [128, D]) for b in range(2)]
        w_lo = [own(f"w_lo{b}", o_w[b], [128, D]) for b in range(2)]
        xl = tiles(o_c, KD, HN + 1, 128)
        gates = tiles(o_c + KD * (HN + 1), KD, HN, 128)
        o_mixt = o_c + KD * (2 * HN + 1)
        mixt = [at(o_mixt + b * HN, HN, 128) for b in range(2)]
        yl = [at(o_f, D), at(o_f + D, D)] + [at(NT * PADN + i * D, D) for i in range(HT - 2)]
        turn_banks = [(6, 7), (0, 1), (2, 5)]
        assert (HT - 2) * D <= NT * N // 2

        def place(c):
            return c if c < HT else 0

        def banks_of(c):
            return turn_banks[place(c) % 3]

        prod = [at(o_f + D + b * HN, HN, 128) for b in range(2)]
        assert o_mixed + 2 * HP <= o_w[0] and o_w[0] + D <= o_a
        assert o_xop[1] + 2 * KD * HP <= SPLIT and o_mixt + 2 * HN <= o_e + 2 * D
        assert aligned(o_e + 2 * D) + 2 * D <= o_f and o_w[1] + D <= ARENA

        ident = sb("ident", [128, 128])
        identb = sb("identb", [128, 128], BF16)
        ones = sb("ones", [128, 128])
        iota = sb("iota", [128, NT * W], BF16)
        win_start = sb("win_start", [128, NWIN])
        st = sb("st", [128, 12])
        mv = sb("mv", [128, 2])
        std = sb("std", [128, 1])
        rstd = sb("rstd", [128, 1])
        eps = sb("eps", [128, 1])
        flag = sb("flag", [128, 4])
        npass_i = sb("npass_i", [128, 1], I32)
        benc_c = sb("benc_c", [128, MB])
        deg_c = sb("deg_c", [128, NT])
        dis_c = sb("dis_c", [128, NT])
        amax = sb("amax", [128, 1])
        lscale = sb("lscale", [128, NT])
        linv = sb("linv", [128, NT])
        magic = sb("magic", [128, 2])
        dot_a = sb("dot_a", [128, NT])
        dot_b = sb("dot_b", [128, NT])
        bias_b = sb("bias_b", [128, STEPS * NT])
        bg_row = sb("bg_row", [128, STEPS])
        mu = sb("mu", [128, 4, KD])

        ps = ctx.enter_context(nc.psum_tensor("ps", [128, 8, HALF], F32))

        def bank(i, n=HALF, rows=TN, o=0):
            return ps[0:rows, i, o:o + n]

        def tile_of(a, t):
            return a[:, bass.ds(t, 1), :].rearrange("p a d -> p (a d)")

        ld_edges, ld_enc, ld_conv, ld_lin, ld_dec = (sem("ld_edges"), sem("ld_enc"), sem("ld_conv"),
                                                       sem("ld_lin"), sem("ld_dec"))
        ld_x = [sem("ld_x0"), sem("ld_x1")]
        ld_staged, ld_X = sem("ld_staged"), sem("ld_X")
        ld_raw1 = [sem("ld_raw1_0"), sem("ld_raw1_1")]
        ld_raw2 = [sem("ld_raw2_0"), sem("ld_raw2_1")]
        ld_w1, ld_b1, ld_small, ld_bdec = sem("ld_w1"), sem("ld_b1"), sem("ld_small"), sem("ld_bdec")
        ld_wg = [sem("ld_wg0"), sem("ld_wg1")]
        ld_block = [sem("ld_block0"), sem("ld_block1")]
        consts = sem("consts")
        matrices_zero, plain_ready, part01_ready, part2_ready, deg_rows = (
            sem("matrices_zero"), sem("plain_ready"), sem("part01_ready"), sem("part2_ready"), sem("deg_rows"))
        ln_var, ln_std, ln_step, ln_out = sem("ln_var"), sem("ln_std"), sem("ln_step"), sem("ln_out")
        turned, turned_out = sem("turned"), sem("turned_out")
        prep, prep_max, npass_set, window_set = sem("prep"), sem("prep_max"), sem("npass_set"), sem("window_set")
        hot_ready, chunk_sum, chunk_added, edges_done = (sem("hot_ready"), sem("chunk_sum"), sem("chunk_added"),
                                                         sem("edges_done"))
        deg_sum, deg_col, deg_root, dis_set = sem("deg_sum"), sem("deg_col"), sem("deg_root"), sem("dis_set")
        counts_set = sem("counts_set")
        mm, mm_out = sem("mm"), sem("mm_out")
        dec_mm, dec_out, xb_ready = sem("dec_mm"), sem("dec_out"), sem("xb_ready")
        rabs, rmax, rmax_all, rscale, rmul, rround, rq = (sem("rabs"), sem("rmax"), sem("rmax_all"), sem("rscale"), sem("rmul"),
                                                    sem("rround"), sem("rq"))
        q_step, q_rounded, q_turned, q_copied = sem("q_step"), sem("q_rounded"), sem("q_turned"), sem("q_copied")
        int_mm, int_scaled, x2_ready = sem("int_mm"), sem("int_scaled"), sem("x2_ready")
        g0_mm, g0_out, g0_added, dots = sem("g0_mm"), sem("g0_out"), sem("g0_added"), sem("dots")
        bias_set, diag_set, a_row, tanh_out = sem("bias_set"), sem("diag_set"), sem("a_row"), sem("tanh_out")
        m_set, hi_set, lo_set, g_hi_set, g_lo_set = (sem("m_set"), sem("hi_set"), sem("lo_set"), sem("g_hi_set"),
                                                     sem("g_lo_set"))
        slot_free, g_mm, g_out, x3_ready = sem("slot_free"), sem("g_mm"), sem("g_out"), sem("x3_ready")
        mu_set, part_mix, mix_set, x_hi_set, x_lo_set = (sem("mu_set"), sem("part_mix"), sem("mix_set"),
                                                         sem("x_hi_set"), sem("x_lo_set"))
        half_turned, half_copied, col_set = sem("half_turned"), sem("half_copied"), sem("col_set")
        zero_col = sem("zero_col")
        w_hi_set, w_lo_set, block_mm = sem("w_hi_set"), sem("w_lo_set"), sem("block_mm")
        relu_set = sem("relu_set")
        gate_set, act_set, act_hi_set, act_lo_set = (sem("gate_set"), sem("act_set"), sem("act_hi_set"),
                                                     sem("act_lo_set"))
        prod_set, turned_back, y_out = sem("prod_set"), sem("turned_back"), sem("y_out")
        stored = sem("stored")

        x_t = x.rearrange("(t p) d -> p t d", p=TN)
        out_t = out.rearrange("(t p) d -> p t d", p=TN)
        rhs_t = rhs.rearrange("(k p) n -> p k n", p=128)

        NG = 12 + NT + 12
        NM = STEPS * PARTS
        part_list = [(g, t0, cnt, s) for g, (t0, cnt) in enumerate(GROUPS) for s in range(NT)]

        block = ctx.enter_context(nc.Block())

        @block.sync
        def _(sp):
            sp.dma_start(e_int[:, 0, :], src).then_inc(ld_edges, 16)
            sp.dma_start(e_int[:, 1, :], dst).then_inc(ld_edges, 16)
            sp.dma_start(e_w, edge_w).then_inc(ld_edges, 16)
            for t in range(NT):
                if t >= 2:
                    sp.wait_ge(ln_out, t - 1)
                sp.dma_start(xin[t % 2], x_t[:, t, :]).then_inc(ld_x[t % 2], 16)
                if t == EARLY - 1:
                    sp.dma_start(wenc, wenc_t.rearrange("(k p) m -> p k m", p=128)).then_inc(ld_enc, 16)
                    sp.dma_start(benc_c[0:TN, :], benc).then_inc(ld_enc, 16)
            sp.dma_start(bg_row[0:TN, :], bg.partition_broadcast(TN)).then_inc(ld_small, 16)
            sp.dma_start(mu[:, 0, :], mu_r).then_inc(ld_small, 16)
            sp.dma_start(mu[:, 1, :], mu_k).then_inc(ld_small, 16)
            sp.wait_ge(ln_out, NT)
            sp.dma_start(convw, conv.rearrange("(k p) m -> p k m", p=TN)).then_inc(ld_conv, 16)
            sp.wait_ge(edges_done, 1)
            sp.dma_start(linw, lin_t.rearrange("(k p) m -> p k m", p=TN)).then_inc(ld_lin, 16)
            sp.dma_start(bdec_row, bdec.partition_broadcast(TN)).then_inc(ld_bdec, 16)
            sp.wait_ge(mm, 12)
            sp.dma_start(wdec, wdec_t.rearrange("(k p) m -> p k m", p=TN)).then_inc(ld_dec, 16)
            sp.wait_ge(mm, 12 + NT)
            for k in range(KD):
                if k >= 2:
                    sp.wait_ge(rmax, k - 1)
                sp.dma_start(raw1[k % 2], rhs_t[:, k, :]).then_inc(ld_raw1[k % 2], 16)
            sp.wait_ge(counts_set, NT + 1)
            sp.dma_start(x_staged, x_t[:, 0:STAGED, :]).then_inc(ld_staged, 16)
            sp.wait_ge(mm, NG)
            sp.dma_start(X[:, STAGED:, :], x_t[:, STAGED:, :]).then_inc(ld_X, 16)
            for k in range(KD):
                if k >= 2:
                    sp.wait_ge(rq, k - 1)
                sp.dma_start(raw2[k % 2], rhs_t[:, k, :]).then_inc(ld_raw2[k % 2], 16)
            sp.wait_ge(dec_mm, 2 * NT)
            sp.dma_start(w1, W1.rearrange("(k p) m -> p k m", p=128)).then_inc(ld_w1, 16)
            sp.wait_ge(q_turned, NT)
            sp.dma_start(b1_row, b1.partition_broadcast(TN)).then_inc(ld_b1, 16)
            sp.wait_ge(xb_ready, NT)
            sp.dma_start(wg_row[0], Wg[0].partition_broadcast(TN)).then_inc(ld_wg[0], 16)
            sp.wait_ge(int_scaled, 2 * NT)
            sp.dma_start(wg_row[1], Wg[1].partition_broadcast(TN)).then_inc(ld_wg[1], 16)
            sp.wait_ge(g0_out, NT)
            for b in range(2):
                sp.dma_start(w_raw[b][:], W_ffn[b]).then_inc(ld_block[b], 16)
            for k in range(2, STEPS):
                sp.wait_ge(dots, 2 * NT * (k - 1))
                sp.dma_start(wg_row[k % 2], Wg[k].partition_broadcast(TN)).then_inc(ld_wg[k % 2], 16)

            def load_weights(half, first):
                with sp.Fori(first, BLOCKS - 1, 2) as i:
                    for b in range(2):
                        sp.wait_ge(w_lo_set, half * BLOCKS + i + b - 1)
                        sp.dma_start(w_raw[b][:], W_ffn[bass.ds(i + b, 1)].rearrange("a p m -> p (a m)")
                                     ).then_inc(ld_block[b], 16)

            def store(half, d0, d1):
                sp.wait_ge(y_out, 2 * (half * KD + d1))
                nodes, columns = slice(half * HT, (half + 1) * HT), slice(d0 * 128, d1 * 128)
                sp.dma_start(out_t[:, nodes, columns], X[:, nodes, columns]).then_inc(stored, 16)

            load_weights(0, 2)
            load_weights(1, 0)
            store(0, 0, KD)
            for d0, d1 in STORES:
                store(1, d0, d1)
            sp.wait_ge(stored, 16 * (1 + len(STORES)))

        @block.gpsimd
        def _(pool):
            pool.memset(eps[:], EPS).then_inc(consts, 1)
            pool.memset(ones[:], 1.0).then_inc(consts, 1)
            pool.memset(magic[:, 0:1], MAGIC).then_inc(consts, 1)
            pool.memset(magic[:, 1:2], -MAGIC).then_inc(consts, 1)
            pool.memset(ident[:], 0.0).then_inc(consts, 1)
            pool.memset(identb[:], 0.0).then_inc(consts, 1)
            pool.wait_ge(consts, 6)
            for m in (ident, identb):
                pool.affine_select(out=m[:], in_=m[:], compare_op=ALU.not_equal, fill=1.0, base=0,
                                   pattern=[[-1, 128]], channel_multiplier=1).then_inc(consts, 1)
            pool.iota(iota[:], [[1, NT * W]], base=0, channel_multiplier=0,
                      allow_small_or_imprecise_dtypes=True).then_inc(consts, 1)
            pool.iota(win_start[:], [[W, NWIN]], base=0, channel_multiplier=0,
                      allow_small_or_imprecise_dtypes=True).then_inc(consts, 1)
            pool.wait_ge(prep, 3)
            pool.partition_all_reduce(reduced, extremes, TN, bass.bass_isa.ReduceOp.max).then_inc(prep_max, 1)
            pool.memset(edges[:, 0:NT, :], 0.0).then_inc(matrices_zero, 1)
            pool.memset(edges[:, NT:, :], 0.0).then_inc(matrices_zero, 1)
            pool.wait_ge(npass_set, 1)
            npass = pool.value_load(npass_i[0:1, 0:1], min_val=1, max_val=NWIN)
            with pool.Fori(0, npass) as j:
                with pool.Fori(0, CH - SLOTS + 1, SLOTS) as c:
                    for b in range(SLOTS):
                        pool.wait_ge(plain_ready, j * CH + c + b + 1)
                        pool.tensor_tensor(lo_hot[b][:, 2, 0:TN], lo_hot[b][:, 3, 0:TN],
                                           w_part[:, 2, bass.ds(c + b, 1)].to_broadcast([TN, TN]),
                                           ALU.mult).then_inc(part2_ready, 1)
            pool.wait_ge(edges_done, 1)
            pool.tensor_tensor(deg_sum_rows, counts[:, 0, 0:N], counts[:, 1, 0:N], ALU.add).then_inc(deg_rows, 1)
            for s in range(2, NT):
                pool.wait_ge(deg_rows, s - 1)
                pool.tensor_tensor(deg_sum_rows, deg_sum_rows, counts[:, s, 0:N], ALU.add).then_inc(deg_rows, 1)
            pool.wait_ge(rmax, KD)
            pool.wait_ge(counts_set, 2)
            pool.partition_all_reduce(inv_row, rs_row, 128, bass.bass_isa.ReduceOp.absmax).then_inc(rmax_all, 1)

            pool.wait_ge(ld_bdec, 16)
            pool.wait_ge(rscale, 2)
            for t in range(NT):
                if t < STAGED:
                    pool.wait_ge(ld_staged, 16)
                    xt = x_staged[:, t, :]
                else:
                    pool.wait_ge(ld_X, 16)
                    xt = X[:, t, :]
                pool.tensor_tensor(xt, xt, bdec_row, ALU.add).then_inc(xb_ready, 1)
                if t < KD:
                    pool.wait_ge(ld_raw2[t % 2], 16 * (t // 2 + 1))
                    pool.tensor_tensor(raw2[t % 2], raw2[t % 2], inv_row, ALU.mult).then_inc(rmul, 1)
            with pool.Fori(0, NT) as t:
                pool.wait_ge(g0_out, t + 1)
                xt = X[:, bass.ds(t, 1), 0:H].rearrange("p a d -> p (a d)")
                pool.tensor_tensor(xt, xt, tile_of(state, t), ALU.add).then_inc(g0_added, 1)
            def low_part(k, p):
                m = slice(0, part_list[p][2] * TN)
                pool.wait_ge(hi_set, k * PARTS + p + 1)
                pool.tensor_tensor(m_lo[0:TN, p % RING, m], m_scratch[0:TN, p % RING, m],
                                   m_hi[0:TN, p % RING, m].bitcast(F32), ALU.subtract).then_inc(lo_set, 1)

            def low_weights(i, b):
                pool.wait_ge(w_hi_set, i + 1)
                pool.tensor_tensor(w_lo[b][:], w_raw[b][:], w_hi[b][:].bitcast(F32), ALU.subtract).then_inc(w_lo_set, 1)

            def add_state(t):
                pool.wait_ge(g_out, (STEPS - 1) * NT + t + 1)
                pool.tensor_tensor(X[:, t, H:D], X[:, t, H:D], state[:, t, :], ALU.add).then_inc(x3_ready, 1)

            with pool.Fori(0, STEPS - 1) as k:
                for p in range(PARTS):
                    low_part(k, p)
            for b in range(2):
                low_weights(b, b)
            for p in range(PARTS):
                low_part(STEPS - 1, p)
                if NT + RING < p <= NT + RING + 4:
                    add_state(p - NT - RING - 1)
            for t in range(4, NT):
                add_state(t)
            with pool.Fori(2, HALVES * BLOCKS - 1, 2) as i:
                for b in range(2):
                    low_weights(i + b, b)

        @block.vector
        def _(dve):
            def variance(xt, n):
                dve.bn_stats(st[0:TN, 0:6], xt[:, 0:HALF]).then_inc(ln_step, 1)
                dve.bn_stats(st[0:TN, 6:12], xt[:, HALF:D]).then_inc(ln_step, 1)
                dve.wait_ge(ln_step, n * 3 + 2)
                dve.bn_aggr(mv[0:TN, :], st[0:TN, :]).then_inc(ln_var, 1)

            def inverse_deviation(n):
                dve.wait_ge(ln_std, n + 1)
                dve.reciprocal(rstd[0:TN, :], std[0:TN, :]).then_inc(ln_step, 1)
                dve.wait_ge(ln_step, n * 3 + 3)

            def stats(xt, n):
                variance(xt, n)
                inverse_deviation(n)

            def normalise(dst_ap, xt):
                dve.tensor_scalar(dst_ap, xt, mv[0:TN, 0:1], rstd[0:TN, :],
                                  ALU.subtract, ALU.mult).then_inc(ln_out, 1)

            dve.wait_ge(consts, 10)
            count = [0]

            def then(ins):
                count[0] += 1
                ins.then_inc(prep, 1)
                dve.wait_ge(prep, count[0])

            dve.wait_ge(ld_edges, 48)
            then(dve.tensor_copy(e_f, e_int))
            then(dve.tensor_copy(extremes[:, 0, :], e_f[:, 1, :]))
            then(dve.tensor_scalar(extremes[:, 1, :], e_f[:, 1, :], -1.0, None, ALU.mult))
            then(dve.tensor_scalar(s0, e_f[:, 0, :], 1.0 / TN, 0.5 / TN - 0.5, ALU.mult, ALU.add))
            then(dve.tensor_scalar(s1, s0, MAGIC, None, ALU.add))
            then(dve.tensor_scalar(s2, s1, -MAGIC, None, ALU.add))
            then(dve.scalar_tensor_tensor(src_lo, s2, -float(TN), e_f[:, 0, :], ALU.mult, ALU.add))
            then(dve.tensor_scalar(key0, s2, float(W), 1.0, ALU.mult, ALU.add))
            rest = e_w
            for p in range(3):
                then(dve.tensor_copy(as_bf16, rest))
                then(dve.tensor_copy(w_part[:, p, :], as_bf16))
                if p < 2:
                    left = [s0, s1][p]
                    then(dve.tensor_tensor(left, rest, w_part[:, p, :], ALU.subtract))
                    rest = left
            for t in range(EARLY):
                b = t % 2
                dve.wait_ge(ld_x[b], 16 * (t // 2 + 1))
                stats(xin[b], t)
                if t >= 2:
                    dve.wait_ge(turned, 2 * t - 2)
                normalise(y[b], xin[b])

            dve.wait_ge(prep_max, 1)
            then(dve.tensor_tensor(s0, reduced[:, 0, :], reduced[:, 1, :], ALU.add))
            then(dve.tensor_reduce(flag[0:TN, 0:1], s0, AX.X, ALU.max))
            then(dve.tensor_scalar(flag[0:TN, 1:2], flag[0:TN, 0:1], W - 0.5, None, ALU.is_lt))
            then(dve.tensor_scalar(flag[0:TN, 2:3], flag[0:TN, 1:2], -float(NWIN - 1), float(NWIN),
                                   ALU.mult, ALU.add))
            dve.tensor_copy(npass_i[0:TN, :], flag[0:TN, 2:3]).then_inc(npass_set, 1)
            then(dve.tensor_scalar(s1, reduced[:, 1, :], -1.0, flag[0:TN, 1:2], ALU.mult, ALU.mult))
            then(dve.tensor_scalar(flag[0:TN, 3:4], flag[0:TN, 1:2], -1.0, 1.0, ALU.mult, ALU.add))
            dve.wait_ge(npass_set, 1)
            npass = dve.value_load(npass_i[0:1, 0:1], min_val=1, max_val=NWIN)

            def hots(c, b):
                dve.tensor_scalar(lo_hot[b][:, 3, 0:TN], iota[0:TN, 0:TN], src_lo[:, bass.ds(c, 1)], None,
                                  ALU.is_equal).then_inc(plain_ready, 1)
                dve.tensor_scalar(win_hot[b], iota[0:TN, :], key[:, bass.ds(c, 1)], None,
                                  ALU.is_equal).then_inc(hot_ready, 1)

            start_regs = [dve.alloc_register(f"start{b}") for b in range(SLOTS)]

            def windows_of(c, n):
                dve.reg_load(start_regs[0:n], base_i[0:1, bass.ds(c, n)])
                return [dve.snap(r, min_val=0, max_val=N - 1) for r in start_regs[0:n]]

            def add_chunk(start, b, i, first=False):
                dve.wait_ge(chunk_sum, i + 1)
                if not first:
                    dve.wait_ge(chunk_added, i)
                window = edges[:, :, bass.ds(start, W)]
                dve.tensor_tensor(window, bank(4 + b, 2 * NT * W).rearrange("p (a w) -> p a w", w=W),
                                  window, ALU.add).then_inc(chunk_added, 1)

            def set_window(j):
                in_pass = [0]

                def step(ins):
                    in_pass[0] += 1
                    ins.then_inc(window_set, 1)
                    dve.wait_ge(window_set, j * 9 + in_pass[0])

                step(dve.tensor_scalar(flag[0:TN, 0:1], win_start[0:TN, bass.ds(j, 1)], flag[0:TN, 3:4], None,
                                       ALU.mult))
                step(dve.tensor_scalar(s2, s1, flag[0:TN, 0:1], None, ALU.add))
                step(dve.tensor_copy(base_i, s2))
                step(dve.tensor_tensor(s0, e_f[:, 1, :], s2, ALU.subtract))
                step(dve.tensor_scalar(s2, s0, -0.5, None, ALU.is_gt))
                step(dve.scalar_tensor_tensor(s2, s0, W - 0.5, s2, ALU.is_lt, ALU.mult))
                step(dve.tensor_tensor(s0, s0, key0, ALU.add))
                step(dve.tensor_tensor(s0, s0, s2, ALU.mult))
                step(dve.tensor_scalar(key, s0, -1.0, None, ALU.add))

            def first_chunks(j):
                for c in range(SLOTS):
                    hots(c, c)
                add_chunk(windows_of(0, 1)[0], 0, j * CH, first=True)

            def other_chunks(j, c0):
                with dve.Fori(c0, CH - SLOTS + 1, SLOTS) as c:
                    starts = windows_of(c - SLOTS + 1, SLOTS)
                    for b in range(SLOTS):
                        hots(c + b, b)
                        add_chunk(starts[b], (b + 1) % SLOTS, j * CH + c + b - SLOTS + 1)
                starts = windows_of(CH - SLOTS + 1, SLOTS - 1)
                for c in range(CH - SLOTS + 1, CH):
                    add_chunk(starts[c - (CH - SLOTS + 1)], c % SLOTS, j * CH + c)
                dve.wait_ge(chunk_added, j * CH + CH)

            dve.wait_ge(turned, 2 * EARLY)
            dve.wait_ge(matrices_zero, 2)
            set_window(0)
            first_chunks(0)
            for c in range(SLOTS, UNROLLED):
                if c % SLOTS == 0:
                    starts = windows_of(c - SLOTS + 1, SLOTS)
                hots(c, c % SLOTS)
                add_chunk(starts[c % SLOTS], (c + 1) % SLOTS, c - SLOTS + 1)
                for t, at_chunk in LN_AT.items():
                    if c == at_chunk:
                        dve.wait_ge(ld_x[t % 2], 16 * (t // 2 + 1))
                        variance(xin[t % 2], t)
                    if c == at_chunk + 1:
                        inverse_deviation(t)
                        dve.wait_ge(turned, 2 * t)
                        normalise(y[0], xin[t % 2])
            other_chunks(0, UNROLLED)
            with dve.If(npass > 1):
                with dve.Fori(1, npass) as j:
                    set_window(j)
                    first_chunks(j)
                    other_chunks(j, SLOTS)
            dve.memset(flag[0:TN, 0:1], 0.0).then_inc(edges_done, 1)

            for k in range(KD):
                dve.wait_ge(rabs, k + 1)
                if k == 0:
                    dve.tensor_copy(rs_row, raw1[0]).then_inc(rmax, 1)
                else:
                    dve.wait_ge(rmax, k)
                    dve.tensor_tensor(rs_row, raw1[k % 2], rs_row, ALU.max).then_inc(rmax, 1)

            dve.wait_ge(deg_sum, 1)
            dve.tensor_scalar(deg_c[0:TN, :], bank(4, NT), 1.0, None, ALU.max).then_inc(deg_col, 1)
            dve.wait_ge(deg_root, 1)
            dve.reciprocal(dis_c[0:TN, :], deg_c[0:TN, :]).then_inc(dis_set, 1)
            dve.wait_ge(dis_set, 1)
            dve.tensor_copy(first_counts, counts[:, 0, 0:N]).then_inc(counts_set, 1)
            dve.wait_ge(counts_set, 1)
            dve.tensor_copy(counts16[:, 0, :], first_counts).then_inc(counts_set, 1)
            for t in range(1, NT):
                dve.wait_ge(counts_set, t + 1)
                dve.tensor_copy(counts16[:, t, :], counts[:, t, 0:N]).then_inc(counts_set, 1)

            dve.wait_ge(rmax_all, 1)
            dve.tensor_scalar(rs_row, inv_row, 1e-12, 1.0 / 127.0, ALU.max, ALU.mult).then_inc(rscale, 1)
            dve.wait_ge(rscale, 1)
            dve.reciprocal(inv_row, rs_row).then_inc(rscale, 1)

            for t in range(NT):
                xt = X[:, t, :]
                dve.wait_ge(xb_ready, t + 1)
                for h in range(2):
                    dve.wait_ge(dec_mm, 2 * t + h + 1)
                    col = slice(h * HALF, (h + 1) * HALF)
                    xb = x_staged[:, t, col] if t < STAGED else xt[:, col]
                    dve.tensor_tensor(xt[:, col], bank(2 * (t % 2) + h), xb, ALU.add).then_inc(dec_out, 1)
                dve.wait_ge(dec_out, 2 * t + 2)
                stats(xt, t + NT)
                if t >= 2:
                    dve.wait_ge(q_rounded, 2 * t - 2)
                normalise(y[t % 2], xt)
                dve.wait_ge(ln_out, t + NT + 1)
                dve.tensor_reduce(amax[0:TN, :], y[t % 2], AX.X, ALU.max,
                                  apply_absolute_value=True).then_inc(q_step, 1)
                dve.wait_ge(q_step, 3 * t + 1)
                dve.tensor_scalar(lscale[0:TN, t:t + 1], amax[0:TN, :], 1e-12, 1.0 / 127.0, ALU.max,
                                  ALU.mult).then_inc(q_step, 1)
                dve.wait_ge(q_step, 3 * t + 2)
                dve.reciprocal(linv[0:TN, t:t + 1], lscale[0:TN, t:t + 1]).then_inc(q_step, 1)

            def dot_products(gt, k, t):
                for i, (dot, junk) in enumerate(((dot_a, tmp[0]), (dot_b, tmp[1]))):
                    dve.tensor_tensor_reduce(junk, gt, wg_row[k % 2][:, i * H:(i + 1) * H], 1.0, 0.0,
                                             ALU.mult, ALU.add, dot[0:TN, t:t + 1]).then_inc(dots, 1)

            def integer_tile(t):
                if t > 2:
                    dve.wait_ge(dots, 2 * t - 4)
                for h in range(2):
                    dve.wait_ge(int_mm, 2 * t + h + 1)
                    if t:
                        dve.wait_ge(x2_ready, 2 * t + h - 1)
                    dve.scalar_tensor_tensor(tmp[h], bank(h), lscale[0:TN, t:t + 1],
                                             rs_row[0:TN, h * HALF:(h + 1) * HALF], ALU.mult,
                                             ALU.mult).then_inc(int_scaled, 1)
                    dve.wait_ge(int_scaled, 2 * t + h + 1)
                    xh = X[:, t, h * HALF:(h + 1) * HALF]
                    dve.tensor_tensor(xh, xh, tmp[h], ALU.add).then_inc(x2_ready, 1)
                dve.wait_ge(x2_ready, 2 * t + 2)
                stats(X[:, t, :], t + 2 * NT)
                if t == 0:
                    dve.wait_ge(q_rounded, 2 * NT)
                dve.wait_ge(turned, 2 * NT + 2 * t)
                normalise(y[1], X[:, t, :])

            def graph_input(t):
                if t == 0:
                    dve.wait_ge(ld_wg[0], 16)
                    dve.wait_ge(ld_b1, 16)
                dve.wait_ge(g0_mm, t + 1)
                dve.tensor_tensor(state[:, t, :], bank(4), b1_row, ALU.add).then_inc(g0_out, 1)
                dve.wait_ge(g0_out, t + 1)
                dve.wait_ge(x2_ready, 2 * min(t + 3, NT))
                dve.wait_ge(dots, 2 * t)
                dot_products(state[:, t, :], 0, t)

            integer_tile(0)
            integer_tile(1)
            for t in range(2, NT):
                integer_tile(t)
                graph_input(t - 2)
            graph_input(NT - 2)
            graph_input(NT - 1)

            def bias_and_diag(k, t0, cnt):
                dve.wait_ge(dots, 2 * (NT * k + t0 + cnt))
                dve.tensor_scalar(bias_b[0:TN, k * NT + t0:k * NT + t0 + cnt], dot_b[0:TN, t0:t0 + cnt], bg_row[0:TN, k:k + 1], None,
                                  ALU.add).then_inc(bias_set, 1)
                for t in range(t0, t0 + cnt):
                    dve.tensor_scalar(diag[:, t, :], ident[0:TN, 0:TN], dot_a[0:TN, t:t + 1], None,
                                      ALU.mult).then_inc(diag_set, 1)

            def matrix_part(k, p):
                g, t0, cnt, s = part_list[p]
                dve.wait_ge(tanh_out, k * PARTS + p + 1)
                m = m_scratch[0:TN, p % RING, 0:cnt * TN]
                dve.tensor_tensor(m, m, counts16[:, s, t0 * TN:(t0 + cnt) * TN], ALU.mult).then_inc(m_set, 1)

            def low_state(k, t):
                dve.wait_ge(g_hi_set, k * NT + t + 1)
                dve.scalar_tensor_tensor(g_lo[0:TN, t, :], state[:, t, :], dis_c[0:TN, t:t + 1],
                                         g_hi[0:TN, t, :].bitcast(F32), ALU.mult, ALU.subtract).then_inc(g_lo_set, 1)

            def new_state(k, g):
                t0, cnt = GROUPS[g]
                if k == 0 and g == 0:
                    dve.wait_ge(g0_added, NT)
                for t in range(t0, t0 + cnt):
                    if t < t0 + cnt - 1:
                        dve.wait_ge(g_mm, k * (NT - len(GROUPS)) + t - g + 1)
                    else:
                        dve.wait_ge(slot_free, k * PARTS + (g + 1) * NT)
                    dve.scalar_tensor_tensor(state[:, t, :], bank(t % 5), dis_c[0:TN, t:t + 1], state[:, t, :],
                                             ALU.mult, ALU.add).then_inc(g_out, 1)

            def next_inputs(k, g):
                t0, cnt = GROUPS[g]
                if k + 1 < STEPS:
                    dve.wait_ge(ld_wg[(k + 1) % 2], 16 * ((k + 1) // 2 + 1))
                    for t in range(t0, t0 + cnt):
                        dve.wait_ge(g_out, k * NT + t + 1)
                        dve.wait_ge(dots, 2 * ((k + 1) * NT + t))
                        dot_products(state[:, t, :], k + 1, t)
                    bias_and_diag(k + 1, t0, cnt)

            dve.wait_ge(ld_small, 48)
            for t0, cnt in GROUPS:
                bias_and_diag(0, t0, cnt)
            for k in range(STEPS):
                for p in range(PARTS):
                    if p < NT:
                        low_state(k, p)
                    matrix_part(k, p)
                    if p == 1 and k:
                        next_inputs(k - 1, 1)
                        new_state(k - 1, 2)
                    if p == 6 and k:
                        next_inputs(k - 1, 2)
                    if p == NT + RING - 1:
                        new_state(k, 0)
                        next_inputs(k, 0)
                    if p == 2 * NT + RING - 1:
                        new_state(k, 1)

            dve.tensor_scalar(mu[:, 2:4, :], mu[:, 0:2, :], -1.0, 1.0, ALU.mult, ALU.add).then_inc(mu_set, 1)

            def last_norm(c):
                dve.wait_ge(x3_ready, c + 1)
                stats(X[:, c, :], c + 3 * NT)
                if c >= HT:
                    dve.wait_ge(half_turned, 2 * c)
                normalise(yl[place(c)], X[:, c, :])

            def mix(m):
                which, k = m // KD % 2, m % KD
                dve.wait_ge(part_mix, m + 1)
                if m >= 2:
                    dve.wait_ge(x_lo_set, m - 1)
                dve.scalar_tensor_tensor(mixed[m % 2][:, 0:HN], xl[:, k, 1:HN + 1], mu[:, which, k:k + 1], mixt[m % 2],
                                         ALU.mult, ALU.add).then_inc(mix_set, 1)

            def low_mix(m):
                k, b = m % KD, OPERAND[m // KD]
                dve.wait_ge(x_hi_set, m + 1)
                dve.tensor_tensor(x_lo[b][:, k, :], mixed[m % 2], x_hi[b][:, k, :].bitcast(F32),
                                  ALU.subtract).then_inc(x_lo_set, 1)

            def low_act(j):
                d, (c0, cn), b = j // 2 % KD, HGROUPS[j % 2], j // (2 * KD)
                dve.wait_ge(act_hi_set, j + 1)
                dve.tensor_tensor(x_lo[b][:, d, c0:c0 + cn], mixed[j % 2][:, 0:cn],
                                  x_hi[b][:, d, c0:c0 + cn].bitcast(F32), ALU.subtract).then_inc(act_lo_set, 1)

            def add_back(n):
                half, d = divmod(n, KD)
                dve.wait_ge(turned_back, n + 1)
                col = slice(d * 128, (d + 1) * 128)
                for t0, cnt, b in ((0, 4, 4), (4, HT - 4, 5)):
                    xt = X[:, half * HT + t0:half * HT + t0 + cnt, col]
                    dve.tensor_tensor(xt, xt, bank(b, cnt * 128).rearrange("p (t f) -> p t f", t=cnt),
                                      ALU.add).then_inc(y_out, 1)

            dve.wait_ge(m_set, NM)
            for c in range(HT):
                last_norm(c)
            new_state(STEPS - 1, 2)
            dve.wait_ge(slot_free, NM)
            dve.wait_ge(lo_set, NM)
            dve.memset(xl[:, :, 0:1], 0.0).then_inc(col_set, 1)
            for b in range(2):
                dve.memset(mixed[b][:, HN:HP], 0.0).then_inc(zero_col, 1)
            for m in range(KD):
                mix(m)
                if m:
                    low_mix(m - 1)
            low_mix(KD - 1)
            for half in range(HALVES):
                base = half * BLOCKS
                for d in range(KD):
                    m = (2 * half + 1) * KD + d
                    mix(m)
                    low_mix(m)
                    if half and d == 0:
                        add_back(KD - 1)
                first = half * 2 * KD
                for j in range(first, first + 2 * KD):
                    dve.wait_ge(relu_set, j + 1)
                    relu = mixed[j % 2][:, 0:HGROUPS[j % 2][1]]
                    dve.tensor_tensor(relu, relu, relu, ALU.mult).then_inc(act_set, 1)
                    if j > first:
                        low_act(j - 1)
                low_act(first + 2 * KD - 1)
                for d in range(KD):
                    n = half * KD + d
                    if half == 0 and d < HT:
                        last_norm(HT + d)
                    if half == 0:
                        for k in MIX_AT.get(d, ()):
                            if k == 0:
                                dve.wait_ge(act_lo_set, 2 * KD)
                            mix(2 * KD + k)
                            low_mix(2 * KD + k)
                    for g, (c0, cn) in enumerate(REAL):
                        dve.wait_ge(block_mm, 2 * (base + 2 * KD + d) + g + 1)
                        if d == 0:
                            dve.wait_ge(gate_set, 2 * KD * (half + 1))
                        if n >= 2:
                            dve.wait_ge(turned_back, n - 1)
                        dve.tensor_tensor(prod[n % 2][:, c0:c0 + cn], bank(2 * (d % 2) + g, cn, 128),
                                          gates[:, d, c0:c0 + cn], ALU.mult).then_inc(prod_set, 1)
                    if d:
                        add_back(n - 1)
            add_back(HALVES * KD - 1)

        @block.scalar
        def _(act):
            def root(n):
                act.wait_ge(ln_var, n + 1)
                act.activation(std[0:TN, :], mv[0:TN, 1:2], ACT.Sqrt, bias=eps[0:TN, :]).then_inc(ln_std, 1)

            act.wait_ge(consts, 10)
            def turned_copy(t, half, b):
                act.wait_ge(turned, 2 * t + half + 1)
                act.activation(xlnT[:, 4 * half:4 * half + 4, t * TN:(t + 1) * TN],
                               bank(b, 4 * TN, 128).rearrange("p (k n) -> p k n", k=4),
                               ACT.Copy).then_inc(turned_out, 1)

            for t in range(EARLY):
                root(t)
                for half in range(2):
                    turned_copy(t, half, 2 * (t % 2) + half)

            def weigh(c, b, i):
                act.wait_ge(plain_ready, i + 1)
                for p in range(2):
                    last = act.activation(lo_hot[b][:, p, 0:TN], lo_hot[b][:, 3, 0:TN], ACT.Copy,
                                          scale=w_part[:, p, bass.ds(c, 1)])
                last.then_inc(part01_ready, 1)

            def group_out(n):
                act.wait_ge(mm, n + 1)
                if n < 12:
                    c0, cn = COLS[n // MB]
                    m = n % MB
                    act.activation(hT[:, m, c0:c0 + cn], bank(n % 3, cn), ACT.Sigmoid,
                                   bias=benc_c[0:TN, m:m + 1]).then_inc(mm_out, 1)
                else:
                    act.activation(h2[:, n - 12, :], bank(n % 3, EMB), ACT.Copy).then_inc(mm_out, 1)

            act.wait_ge(ld_enc, 32)
            n = 0
            for c in range(CH):
                weigh(c, c % SLOTS, c)
                for t, at_chunk in LN_AT.items():
                    if c == at_chunk:
                        root(t)
                    for half in range(2):
                        if c == at_chunk + 3 + half:
                            turned_copy(t, half, 3)
                while n < 12 + NT and group_end(n) * CH <= (c - 2) * DENSE:
                    group_out(n)
                    n += 1
            while n < 12 + NT:
                group_out(n)
                n += 1
            act.wait_ge(npass_set, 1)
            npass = act.value_load(npass_i[0:1, 0:1], min_val=1, max_val=NWIN)
            with act.If(npass > 1):
                with act.Fori(1, npass) as j:
                    with act.Fori(0, CH - SLOTS + 1, SLOTS) as c:
                        for b in range(SLOTS):
                            weigh(c + b, b, j * CH + c + b)
            for m in range(MB):
                if m == 1:
                    act.wait_ge(deg_col, 1)
                    act.activation(deg_c[0:TN, :], deg_c[0:TN, :], ACT.Sqrt).then_inc(deg_root, 1)
                for i, (c0, cn) in enumerate(COLS):
                    if m == 0:
                        for k in range(3 * i, min(3 * i + 3, KD)):
                            act.wait_ge(ld_raw1[k % 2], 16 * (k // 2 + 1))
                            act.activation(raw1[k % 2], raw1[k % 2], ACT.Abs).then_inc(rabs, 1)
                    act.wait_ge(mm, n + 1)
                    act.activation(houtT[:, m, c0:c0 + cn], bank(n % 4, cn), ACT.Copy).then_inc(mm_out, 1)
                    n += 1

            def round_tile(t):
                b = t % 2
                act.wait_ge(q_step, 3 * t + 3)
                act.activation(y[b], y[b], ACT.Identity, bias=magic[0:TN, 0:1],
                               scale=linv[0:TN, t:t + 1]).then_inc(q_rounded, 1)
                act.wait_ge(q_rounded, 2 * t + 1)
                if t >= 2:
                    act.wait_ge(q_turned, t - 1)
                act.activation(qtile[b], y[b], ACT.Identity, bias=magic[0:TN, 1:2]).then_inc(q_rounded, 1)

            def round_rhs(k):
                act.wait_ge(rmul, k + 1)
                act.activation(raw2[k % 2], raw2[k % 2], ACT.Identity, bias=magic[:, 0:1]).then_inc(rround, 1)
                act.wait_ge(rround, k + 1)
                act.activation(qR[:, k, :], raw2[k % 2], ACT.Identity, bias=magic[:, 1:2]).then_inc(rq, 1)

            def q_copy(t):
                act.wait_ge(q_turned, t + 1)
                turned_q = ps[:, 4, :].bitcast(BF16)[:, 0:KD * 126].rearrange("p (k n) -> p k n", k=KD)
                act.activation(qT[:, t, :, :], turned_q[:, :, 0:TN], ACT.Copy).then_inc(q_copied, 1)

            root(NT)
            for t in range(NT):
                round_tile(t)
                if t + 1 < NT:
                    root(t + NT + 1)
                if t < KD:
                    round_rhs(t)
                q_copy(t)

            def x_copy(t, first=False):
                for half in range(2):
                    if not first:
                        act.wait_ge(g0_mm, t)
                    act.wait_ge(turned, 2 * NT + 2 * t + half + 1)
                    act.activation(xT[:, 4 * half:4 * half + 4, :],
                                   bank(2 + half, 4 * TN, 128).rearrange("p (k n) -> p k n", k=4),
                                   ACT.Copy).then_inc(turned_out, 1)

            act.wait_ge(rq, KD)
            root(2 * NT)
            root(2 * NT + 1)
            x_copy(0, first=True)
            with act.Fori(1, NT - 1) as t:
                root(t + 2 * NT + 1)
                x_copy(t)
            x_copy(NT - 1)

            def high_weights(i):
                if i >= 2:
                    act.wait_ge(block_mm, 2 * (i - 1))
                act.wait_ge(ld_block[i % 2], 16 * (i // 2 + 1))
                act.activation(w_hi[i % 2][:], w_raw[i % 2][:], ACT.Copy).then_inc(w_hi_set, 1)

            def high_part(k, p, first):
                m = slice(0, part_list[p][2] * TN)
                if p >= RING or not first:
                    act.wait_ge(slot_free, k * PARTS + p - RING + 1)
                act.wait_ge(m_set, k * PARTS + p + 1)
                act.activation(m_hi[0:TN, p % RING, m], m_scratch[0:TN, p % RING, m], ACT.Copy).then_inc(hi_set, 1)

            def step(k, first):
                for p, (g, t0, cnt, s) in enumerate(part_list):
                    if g == 0:
                        if not first:
                            act.wait_ge(g_out, k * NT + s - NT + 1)
                            act.wait_ge(slot_free, k * PARTS + s - NT + 1)
                        act.activation(g_hi[0:TN, s, :], state[:, s, :], ACT.Copy,
                                       scale=dis_c[0:TN, s:s + 1]).then_inc(g_hi_set, 1)
                        for i, (first_source, _) in enumerate(GROUPS):
                            if s == first_source:
                                act.wait_ge(bias_set, k * len(GROUPS) + i + 1)
                    if s == 0:
                        act.wait_ge(a_row, k * len(GROUPS) + g + 1)
                    if p >= RING or not first:
                        act.wait_ge(lo_set, k * PARTS + p - RING + 1)
                    act.activation(m_scratch[0:TN, p % RING, 0:cnt * TN], bank(5 + g, cnt * TN), ACT.Tanh,
                                   bias=bias_b[0:TN, k * NT + s:k * NT + s + 1]).then_inc(tanh_out, 1)
                    if p:
                        high_part(k, p - 1, first)
                high_part(k, PARTS - 1, first)

            act.wait_ge(g0_out, NT)
            for k in range(STEPS):
                step(k, k == 0)
                if k == 0:
                    for b in range(2):
                        high_weights(b)

            def half_copy(c):
                j = c % HT
                for i in range(2):
                    act.wait_ge(half_turned, 2 * c + i + 1)
                    act.activation(xl[:, 4 * i:4 * i + 4, 1 + j * TN:1 + (j + 1) * TN],
                                   bank(banks_of(c)[i], 4 * TN, 128).rearrange("p (k n) -> p k n", k=4),
                                   ACT.Copy).then_inc(half_copied, 1)

            def mix_term(m):
                which, k = m // KD % 2, m % KD
                if m >= 2:
                    act.wait_ge(mix_set, m - 1)
                act.activation(mixt[m % 2], xl[:, k, 0:HN], ACT.Copy,
                               scale=mu[:, 2 + which, k:k + 1]).then_inc(part_mix, 1)

            def high_mix(m):
                k, b = m % KD, OPERAND[m // KD]
                act.wait_ge(mix_set, m + 1)
                act.activation(x_hi[b][:, k, :], mixed[m % 2], ACT.Copy).then_inc(x_hi_set, 1)

            for c in range(HT):
                root(3 * NT + c)
            act.wait_ge(slot_free, NM)
            act.wait_ge(lo_set, NM)
            for c in range(HT):
                half_copy(c)
            act.wait_ge(mu_set, 1)
            act.wait_ge(zero_col, 2)
            act.wait_ge(col_set, 1)
            act.wait_ge(half_copied, 2 * HT)
            for m in range(KD):
                mix_term(m)
                if m:
                    high_mix(m - 1)
            high_mix(KD - 1)
            for half in range(HALVES):
                base = half * BLOCKS
                for d in range(KD):
                    if base + d:
                        high_weights(base + d + 1)
                    mix_term((2 * half + 1) * KD + d)
                    if d == 0:
                        if half == 0:
                            act.wait_ge(x3_ready, NT)
                        else:
                            act.wait_ge(block_mm, 2 * BLOCKS)
                    high_mix((2 * half + 1) * KD + d)
                    for g, (c0, cn) in enumerate(REAL):
                        act.wait_ge(block_mm, 2 * (base + d) + g + 1)
                        act.activation(gates[:, d, c0:c0 + cn], bank(2 * (d % 2) + g, cn, 128),
                                       ACT.Sigmoid).then_inc(gate_set, 1)
                first = half * 2 * KD

                def high_act(j):
                    d, (c0, cn) = j // 2 % KD, HGROUPS[j % 2]
                    act.wait_ge(act_set, j + 1)
                    act.activation(x_hi[half][:, d, c0:c0 + cn], mixed[j % 2][:, 0:cn],
                                   ACT.Copy).then_inc(act_hi_set, 1)

                for j in range(first, first + 2 * KD):
                    if j % 2 == 0:
                        high_weights(base + KD + (j - first) // 2 + 1)
                    act.wait_ge(block_mm, 2 * (base + KD) + j - first + 1)
                    if j < first + 2:
                        act.wait_ge(x_lo_set, (2 * half + 2) * KD)
                    else:
                        act.wait_ge(act_lo_set, j - 1)
                    cn = HGROUPS[j % 2][1]
                    act.activation(mixed[j % 2][:, 0:cn], bank(j % 4, cn, 128), ACT.Relu).then_inc(relu_set, 1)
                    if j > first:
                        high_act(j - 1)
                high_act(first + 2 * KD - 1)
                for d in range(KD):
                    if half == 0 and d < HT:
                        root(3 * NT + HT + d)
                    if base + 2 * KD + d + 1 < HALVES * BLOCKS:
                        high_weights(base + 2 * KD + d + 1)
                    if half == 0:
                        if d == 0:
                            act.wait_ge(mix_set, 2 * KD)
                            act.activation(xl[:, :, 0], xl[:, :, HN], ACT.Copy).then_inc(col_set, 1)
                            act.wait_ge(col_set, 2)
                        if d < HT:
                            half_copy(HT + d)
                        for k in MIX_AT.get(d, ()):
                            if k == 0:
                                act.wait_ge(half_copied, 4 * HT)
                            mix_term(2 * KD + k)
                            high_mix(2 * KD + k)

        @block.tensor
        def _(pe):
            def turn(tile, banks, done):
                for half in range(2):
                    for k in range(4):
                        f = 4 * half + k
                        t = pe.transpose(bank(banks[half], TN, 128, k * TN), tile[:, f * 128:(f + 1) * 128],
                                         ident[0:TN, 0:TN])
                    t.then_inc(done, 1)

            pe.wait_ge(consts, 10)
            for t in range(EARLY):
                b = t % 2
                pe.wait_ge(ln_out, t + 1)
                if t >= 2:
                    pe.wait_ge(turned_out, 2 * t - 2)
                turn(y[b], (2 * b, 2 * b + 1), turned)

            def turn_beside(t, half):
                pe.wait_ge(ln_out, t + 1)
                pe.wait_ge(turned_out, 2 * t + half)
                for k in range(4):
                    f = 4 * half + k
                    last = pe.transpose(bank(3, TN, 128, k * TN), y[0][:, f * 128:(f + 1) * 128], ident[0:TN, 0:TN])
                last.then_inc(turned, 1)

            def chunk_product(b, i):
                pe.wait_ge(part01_ready, i + 1)
                pe.wait_ge(part2_ready, i + 1)
                pe.wait_ge(hot_ready, i + 1)
                for p in range(3):
                    pe.matmul(bank(4 + b, NT * W), lo_hot[b][:, p, 0:TN], win_hot[b],
                              start=(p == 0), stop=(p == 2), skip_group_check=True)
                pe.matmul(bank(4 + b, NT * W, TN, NT * W), lo_hot[b][:, 3, 0:TN], win_hot[b],
                          start=False, stop=True, skip_group_check=True).then_inc(chunk_sum, 1)

            def dense_product(i):
                if i < 12 * KD:
                    n, k = divmod(i, KD)
                    c0, cn = COLS[n // MB]
                    m = n % MB
                    if i == 0:
                        pe.wait_ge(ld_enc, 32)
                    if k == 0 and m == 0:
                        pe.wait_ge(turned_out, 2 * tiles_for(c0 + cn))
                    if k == 0 and n >= 3:
                        pe.wait_ge(mm_out, n - 2)
                    last = pe.matmul(bank(n % 3, cn), wenc[:, k, m * TN:(m + 1) * TN],
                                     xlnT[:, k, c0:c0 + cn], start=(k == 0), stop=(k == KD - 1))
                    if k == KD - 1:
                        last.then_inc(mm, 1)
                else:
                    t, k = divmod(i - 12 * KD, MB)
                    n = 12 + t
                    if t == 0 and k == 0:
                        pe.wait_ge(ld_conv, 16)
                        pe.wait_ge(mm_out, 12)
                    elif k == 0:
                        pe.wait_ge(mm_out, n - 2)
                    last = pe.matmul(bank(n % 3, EMB), hT[:, k, t * TN:(t + 1) * TN], convw[:, k, :],
                                     start=(k == 0), stop=(k == MB - 1))
                    if k == MB - 1:
                        last.then_inc(mm, 1)

            for c in range(CH):
                if c >= SLOTS:
                    pe.wait_ge(chunk_added, c - SLOTS + 1)
                chunk_product(c % SLOTS, c)
                for i in range(c * DENSE // CH, (c + 1) * DENSE // CH):
                    dense_product(i)
                for t, at_chunk in LN_AT.items():
                    for half in range(2):
                        if c == at_chunk + 2 + half:
                            turn_beside(t, half)
            pe.wait_ge(npass_set, 1)
            npass = pe.value_load(npass_i[0:1, 0:1], min_val=1, max_val=NWIN)
            with pe.If(npass > 1):
                with pe.Fori(1, npass) as j:
                    with pe.Fori(0, CH - SLOTS + 1, SLOTS) as c:
                        for b in range(SLOTS):
                            pe.wait_ge(chunk_added, j * CH + c + b - SLOTS + 1)
                            chunk_product(b, j * CH + c + b)

            def degrees():
                pe.wait_ge(deg_rows, NT - 1)
                for t in range(NT):
                    last = pe.matmul(bank(4, 1, TN, t), deg_sum_rows[:, t * TN:(t + 1) * TN], ones[0:TN, 0:1],
                                     start=True, stop=True, skip_group_check=True)
                last.then_inc(deg_sum, 1)

            pe.wait_ge(edges_done, 1)
            n = 12 + NT
            pe.wait_ge(mm_out, n)
            for m in range(MB):
                for i, (c0, cn) in enumerate(COLS):
                    pe.wait_ge(mm_out, n - 3)
                    for s in range(NT):
                        pe.matmul(bank(n % 4, cn), h2[:, s, m * TN:(m + 1) * TN],
                                  edges[:, s, c0:c0 + cn], start=(s == 0), stop=False)
                    if n == 12 + NT:
                        pe.wait_ge(ld_lin, 16)
                    for k in range(MB):
                        last = pe.matmul(bank(n % 4, cn), linw[:, k, m * TN:(m + 1) * TN], hT[:, k, c0:c0 + cn],
                                         start=False, stop=(k == MB - 1))
                    last.then_inc(mm, 1)
                    n += 1
                    if (m, i) == (1, 0):
                        degrees()

            def turn_q(t):
                pe.wait_ge(q_rounded, 2 * t + 2)
                if t:
                    pe.wait_ge(q_copied, t)
                for f in range(KD):
                    last = pe.transpose(ps[:, 4, :].bitcast(BF16)[:, f * 126:f * 126 + TN],
                                        qtile[t % 2][:, f * 128:(f + 1) * 128], identb[0:TN, 0:TN])
                last.then_inc(q_turned, 1)

            pe.wait_ge(ld_dec, 16)
            pe.wait_ge(mm_out, NG)
            for t in range(NT):
                for h in range(2):
                    if t >= 2:
                        pe.wait_ge(dec_out, 2 * (t - 2) + h + 1)
                    for k in range(MB):
                        last = pe.matmul(bank(2 * (t % 2) + h), houtT[:, k, t * TN:(t + 1) * TN],
                                         wdec[:, k, h * HALF:(h + 1) * HALF], start=(k == 0), stop=(k == MB - 1))
                    last.then_inc(dec_mm, 1)
                if t:
                    turn_q(t - 1)

            def integer_product(t):
                pe.wait_ge(q_copied, t + 1)
                pe.wait_ge(int_scaled, 2 * t)
                for h in range(2):
                    for k in range(KD):
                        lhs = qT[:, bass.ds(t, 1), k, :].rearrange("p t n -> p (t n)")
                        last = pe.matmul(bank(h), lhs, qR[:, k, h * HALF:(h + 1) * HALF],
                                         start=(k == 0), stop=(k == KD - 1))
                    last.then_inc(int_mm, 1)

            def graph_input(t, first=False):
                pe.wait_ge(turned_out, 2 * NT + 2 * t + 2)
                if not first:
                    pe.wait_ge(g0_out, t)
                for k in range(KD):
                    last = pe.matmul(bank(4), xT[:, k, :], w1[:, k, :], start=(k == 0), stop=(k == KD - 1))
                last.then_inc(g0_mm, 1)

            def turn_x(t):
                pe.wait_ge(ln_out, 2 * NT + t + 1)
                pe.wait_ge(turned_out, 2 * NT + 2 * t)
                turn(y[1], (2, 3), turned)

            pe.wait_ge(rq, KD)
            pe.wait_ge(dec_out, 2 * (NT - 1))
            integer_product(0)
            turn_q(NT - 1)
            pe.wait_ge(dec_out, 2 * NT)
            integer_product(1)
            turn_x(0)
            pe.wait_ge(ld_w1, 16)
            integer_product(2)
            graph_input(0, first=True)
            turn_x(1)
            with pe.Fori(3, NT) as t:
                integer_product(t)
                graph_input(t - 2)
                turn_x(t - 1)
            graph_input(NT - 2)
            turn_x(NT - 1)
            graph_input(NT - 1)

            def target_row(k, g, first):
                t0, cnt = GROUPS[g]
                pe.wait_ge(diag_set, k * NT + t0 + cnt)
                if not first:
                    pe.wait_ge(tanh_out, (k - 1) * PARTS + (g + 1) * NT)
                for d in range(cnt):
                    last = pe.matmul(bank(5 + g, TN, TN, d * TN), ones[0:TN, 0:TN], diag[:, t0 + d, :],
                                     start=True, stop=True, skip_group_check=True)
                last.then_inc(a_row, 1)

            def group_sums(k, g, first, row_beside=None):
                t0, cnt = GROUPS[g]
                for s in range(NT):
                    slot = (g * NT + s) % RING
                    if s == NT // 2 and row_beside is not None:
                        target_row(k, row_beside, first)
                    pe.wait_ge(lo_set, k * PARTS + g * NT + s + 1)
                    if g == 0:
                        pe.wait_ge(g_lo_set, k * NT + s + 1)
                    for d in range(cnt):
                        t = t0 + d
                        if s == 0 and (t >= 5 or not first):
                            pe.wait_ge(g_out, k * NT + t - 4)
                        m = slice(d * TN, (d + 1) * TN)
                        for i, (lhs, rhs_s) in enumerate(((m_hi, g_hi), (m_hi, g_lo), (m_lo, g_hi))):
                            last = pe.matmul(bank(t % 5), lhs[0:TN, slot, m], rhs_s[0:TN, s, :],
                                             start=(s == 0 and i == 0), stop=(s == NT - 1 and i == 2))
                        if s == NT - 1 and d < cnt - 1:
                            last.then_inc(g_mm, 1)
                    last.then_inc(slot_free, 1)

            pe.wait_ge(g0_out, NT)
            for g in range(len(GROUPS)):
                target_row(0, g, True)
            group_sums(0, 0, True)
            group_sums(0, 1, True)
            with pe.Fori(1, STEPS) as k:
                target_row(k, 0, False)
                group_sums(k - 1, 2, False)
                group_sums(k, 0, False, row_beside=1)
                target_row(k, 2, False)
                group_sums(k, 1, False)
            group_sums(STEPS - 1, 2, False)

            def turn_half(c):
                pe.wait_ge(ln_out, c + 3 * NT + 1)
                if c >= 3:
                    pe.wait_ge(half_copied, 2 * (c - 2 if c < HT else c))
                turn(yl[place(c)], banks_of(c), half_turned)

            def block(i, b, operand, bank_free, ready):
                pe.wait_ge(w_lo_set, i + 1)
                for g, (c0, cn) in enumerate(HGROUPS):
                    pe.wait_ge(*bank_free(g))
                    for k in range(KD):
                        if ready:
                            pe.wait_ge(*ready(k, g))
                        w = slice(k * 128, (k + 1) * 128)
                        for j, (lhs, rhs_s) in enumerate(((w_hi, x_hi), (w_hi, x_lo), (w_lo, x_hi))):
                            last = pe.matmul(bank(2 * b + g, cn, 128), lhs[b][:, w],
                                             rhs_s[operand][:, k, c0:c0 + cn],
                                             start=(k == 0 and j == 0), stop=(k == KD - 1 and j == 2))
                    last.then_inc(block_mm, 1)

            def blocks(base, operand, out, count, before, ready, between=None):
                for d in range(2):
                    block(base + d, d, operand, lambda g: before(d, g), ready if d == 0 else None)
                    if d == 0 and between is not None:
                        turn_back(between)
                with pe.Fori(2, KD - 1, 2) as d:
                    for b in range(2):
                        block(base + d + b, b, operand, lambda g: (out, count + 2 * (d + b - 2) + g + 1), None)

            def turn_back(n):
                pe.wait_ge(prod_set, 2 * n + 2)
                if n:
                    pe.wait_ge(y_out, 2 * n)
                for t in range(HT):
                    last = pe.transpose(bank(4 + t // 4, 128, TN, (t % 4) * 128),
                                        prod[n % 2][:, t * TN:(t + 1) * TN], ident[:, :])
                last.then_inc(turned_back, 1)

            pe.wait_ge(tanh_out, NM)
            pe.wait_ge(g_out, STEPS * NT - 2)
            for c in range(HT):
                turn_half(c)
            for half in range(HALVES):
                base, count = half * BLOCKS, half * 2 * KD

                def banks_before(d, g):
                    if half == 0:
                        return g_out, STEPS * NT
                    return prod_set, count - 3 + 2 * d + g

                blocks(base, half, gate_set, count, banks_before,
                       lambda k, g: (x_lo_set, half * 2 * KD + k + 1), KD - 1 if half else None)
                blocks(base + KD, 1 - half, relu_set, count, lambda d, g: (gate_set, count + 2 * (KD - 2 + d) + g + 1),
                       lambda k, g: (x_lo_set, (half * 2 + 1) * KD + k + 1))
                for d in range(KD):
                    def value_banks(g):
                        if d < 2:
                            return relu_set, count + 2 * (KD - 2 + d) + g + 1
                        return prod_set, count + 2 * (d - 2) + g + 1
                    block(base + 2 * KD + d, d % 2, half, value_banks,
                          (lambda k, g: (act_lo_set, count + 2 * k + g + 1)) if d == 0 else None)
                    if d:
                        turn_back(half * KD + d - 1)
                    if half == 0 and d < HT:
                        turn_half(HT + d)
            turn_back(HALVES * KD - 1)


def kernel(x, src, dst, edge_weight, L0_gnn_wenc, L0_gnn_benc, L0_gnn_wdec, L0_gnn_bdec, L0_gnn_conv_weight,
           L0_gnn_lin_weight, L0_ffn_rhs, L1_gnn_W1, L1_gnn_b1, L1_gnn_Wg, L1_gnn_bg, L1_ffn_W_r, L1_ffn_W_k,
           L1_ffn_W_v, L1_ffn_mu_r, L1_ffn_mu_k):
    import numpy as np
    import concourse.bacc as bacc
    from concourse.bass_utils import run_bass_kernel_spmd

    def chunks(a):
        return np.asarray(a).reshape(CH, TN).T

    def blocks(a, p):
        return np.asarray(a).reshape(-1, p).T

    def output_blocks(w):
        return np.asarray(w).reshape(KD, 128, KD, 128).transpose(0, 3, 2, 1).reshape(KD, 128, D)

    arrays = {
        "x": x, "src": chunks(src), "dst": chunks(dst), "edge_w": chunks(edge_weight),
        "wenc_t": np.asarray(L0_gnn_wenc).T, "benc": blocks(L0_gnn_benc, TN),
        "wdec_t": np.asarray(L0_gnn_wdec).T, "bdec": L0_gnn_bdec,
        "conv": L0_gnn_conv_weight, "lin_t": np.asarray(L0_gnn_lin_weight).T, "rhs": L0_ffn_rhs,
        "W1": L1_gnn_W1, "b1": L1_gnn_b1, "Wg": np.asarray(L1_gnn_Wg).reshape(STEPS, 2 * H),
        "bg": np.asarray(L1_gnn_bg).reshape(STEPS),
        "W_ffn": np.concatenate([output_blocks(w) for w in (L1_ffn_W_r, L1_ffn_W_k, L1_ffn_W_v)]),
        "mu_r": blocks(L1_ffn_mu_r, 128), "mu_k": blocks(L1_ffn_mu_k, 128),
    }
    arrays = {k: np.ascontiguousarray(v) for k, v in arrays.items()}
    nc = bacc.Bacc("TRN2", target_bir_lowering=False, num_devices=1)
    args = {k: nc.dram_tensor(f"in_{k}", v.shape, mybir.dt.from_np(v.dtype), kind="ExternalInput").ap()
            for k, v in arrays.items()}
    args["out"] = nc.dram_tensor("out_x", (N, D), F32, kind="ExternalOutput").ap()
    build(nc, **args)
    got = run_bass_kernel_spmd(nc, [{f"in_{k}": v for k, v in arrays.items()}], core_ids=[0])
    return got.results[0]["out_x"]
```
